# Optimizing a Trainium2 kernel written in Bass

```python
import numpy as np
import jax
import jax.numpy as jnp

def _softmax(x, axis=-1):
    return jax.nn.softmax(x, axis=axis)

def _gelu(x):
    return jax.nn.gelu(x, approximate=True)

def _silu(x):
    return jax.nn.silu(x)

def _sigmoid(x):
    return jax.nn.sigmoid(x)

def _layernorm(x, axis=-1, eps=1e-05):
    m = jnp.mean(x, axis=axis, keepdims=True)
    v = jnp.var(x, axis=axis, keepdims=True)
    return (x - m) / jnp.sqrt(v + eps)

def _scatter_add(tgt, idx, src, axis=0):
    return tgt.at[idx].add(src)

def _segment_sum(src, seg, n):
    return jax.ops.segment_sum(src, seg, n)
kernel_name = 'mk_lm_tower_d1_tok_ids256_r4_71ebe9'

def setup_inputs(seed: int=0):
    np.random.seed(seed)
    _w = jnp.asarray

    def _rec_inputs():
        import jax
        import jax.numpy as jnp
        _rk = jax.random.key(seed)
        x = jax.random.randint(jax.random.fold_in(_rk, 1), (8, 512), 0, 12564, jnp.int32)
        return x
    x = _rec_inputs()

    def _L0_tok_setup():
        import jax, jax.numpy as jnp
        import numpy as np
        INP_SIZE = 50257
        HIDDEN = 64
        KSIZE = 9
        B, T = (16, 1024)
        key = jax.random.key(seed)
        k1, k2, k3, k4 = jax.random.split(key, 4)
        x = jax.random.randint(k1, (B, T), 0, INP_SIZE, dtype=jnp.int64 if jax.config.jax_enable_x64 else jnp.int32)
        emb = jax.random.normal(k2, (INP_SIZE, HIDDEN), dtype=jnp.float32) * 0.02
        fan_in = HIDDEN * KSIZE
        bound = 1.0 / np.sqrt(fan_in)
        W = jax.random.uniform(k3, (HIDDEN, HIDDEN, KSIZE), dtype=jnp.float32, minval=-bound, maxval=bound)
        b = jax.random.uniform(k4, (HIDDEN,), dtype=jnp.float32, minval=-bound, maxval=bound)
        return {'x': x, 'emb': emb, 'W': W, 'b': b}
    _L0_tok_all = _L0_tok_setup()
    _L0_tok_in = {k: v for k, v in _L0_tok_all.items() if k in ('emb', 'W', 'b')}
    del _L0_tok_all

    def _L0_attn_setup():
        import jax, jax.numpy as jnp
        import numpy as np
        H, D = (8, 32)
        EPS = 1e-05
        key = jax.random.key(seed)
        ks = jax.random.split(key, 4)
        B, N, C = (2, 512, 64)
        inner = H * D
        return {'node_features': jax.random.normal(ks[0], (B, N, C), jnp.float32), 'ln_gamma': jnp.ones((C,), jnp.float32), 'ln_beta': jnp.zeros((C,), jnp.float32), 'W_qkv': jax.random.normal(ks[1], (3 * inner, C), jnp.float32) * 0.02, 'W_gate': jax.random.normal(ks[2], (inner, C), jnp.float32) * 0.02, 'b_gate': jnp.ones((inner,), jnp.float32), 'W_final': jax.random.normal(ks[3], (C, inner), jnp.float32) * 0.02, 'b_final': jnp.zeros((C,), jnp.float32)}
    _L0_attn_all = _L0_attn_setup()
    _L0_attn_in = {k: v for k, v in _L0_attn_all.items() if k in ('ln_gamma', 'ln_beta', 'W_qkv', 'W_gate', 'b_gate', 'W_final', 'b_final')}
    del _L0_attn_all

    def _L0_ffn_setup():
        import jax, jax.numpy as jnp
        import numpy as np
        B, S, H, F, E, K = (8, 1024, 64, 128, 16, 2)
        EPS = 1e-05
        key = jax.random.key(seed)
        ks = jax.random.split(key, 9)
        sc = 0.02
        return {'x': jax.random.normal(ks[0], (B, S, H), dtype=jnp.float32), 'gate_w': jax.random.normal(ks[1], (H, E), dtype=jnp.float32) * sc, 'gate_b': jnp.zeros((E,), dtype=jnp.float32), 'w1': jax.random.normal(ks[2], (E, H, F), dtype=jnp.float32) * sc, 'b1': jnp.zeros((E, F), dtype=jnp.float32), 'w2': jax.random.normal(ks[3], (E, F, H), dtype=jnp.float32) * sc, 'b2': jnp.zeros((E, H), dtype=jnp.float32), 'gamma': jnp.ones((H,), dtype=jnp.float32), 'beta': jnp.zeros((H,), dtype=jnp.float32)}
    _L0_ffn_all = _L0_ffn_setup()
    _L0_ffn_in = {k: v for k, v in _L0_ffn_all.items() if k in ('gate_w', 'gate_b', 'w1', 'b1', 'w2', 'b2', 'gamma', 'beta')}
    del _L0_ffn_all
    return {'x': x, 'L0_tok_emb': _L0_tok_in['emb'], 'L0_tok_W': _L0_tok_in['W'], 'L0_tok_b': _L0_tok_in['b'], 'L0_attn_ln_gamma': _L0_attn_in['ln_gamma'], 'L0_attn_ln_beta': _L0_attn_in['ln_beta'], 'L0_attn_W_qkv': _L0_attn_in['W_qkv'], 'L0_attn_W_gate': _L0_attn_in['W_gate'], 'L0_attn_b_gate': _L0_attn_in['b_gate'], 'L0_attn_W_final': _L0_attn_in['W_final'], 'L0_attn_b_final': _L0_attn_in['b_final'], 'L0_ffn_gate_w': _L0_ffn_in['gate_w'], 'L0_ffn_gate_b': _L0_ffn_in['gate_b'], 'L0_ffn_w1': _L0_ffn_in['w1'], 'L0_ffn_b1': _L0_ffn_in['b1'], 'L0_ffn_w2': _L0_ffn_in['w2'], 'L0_ffn_b2': _L0_ffn_in['b2'], 'L0_ffn_gamma': _L0_ffn_in['gamma'], 'L0_ffn_beta': _L0_ffn_in['beta']}

def reference(x, L0_tok_emb, L0_tok_W, L0_tok_b, L0_attn_ln_gamma, L0_attn_ln_beta, L0_attn_W_qkv, L0_attn_W_gate, L0_attn_b_gate, L0_attn_W_final, L0_attn_b_final, L0_ffn_gate_w, L0_ffn_gate_b, L0_ffn_w1, L0_ffn_b1, L0_ffn_w2, L0_ffn_b2, L0_ffn_gamma, L0_ffn_beta):
    import jax
    import jax.numpy as jnp

    def _L0_tok_ref(x, emb, W, b):
        import jax, jax.numpy as jnp
        import numpy as np
        INP_SIZE = 50257
        HIDDEN = 64
        KSIZE = 9
        B, T = (16, 1024)
        offsets = jnp.arange(-(KSIZE // 2), KSIZE // 2 + 1)
        idx = jnp.clip(x[..., None] + offsets, 0, INP_SIZE - 1)
        gathered = emb[idx]
        out = jnp.einsum('btkh,ohk->bto', gathered, W) + b
        return out

    def _L0_attn_ref(node_features, ln_gamma, ln_beta, W_qkv, W_gate, b_gate, W_final, b_final):
        import jax, jax.numpy as jnp
        import numpy as np
        H, D = (8, 32)
        EPS = 1e-05
        x = node_features
        B, N, _ = x.shape
        mu = jnp.mean(x, axis=-1, keepdims=True)
        var = jnp.mean(jnp.square(x - mu), axis=-1, keepdims=True)
        normed = (x - mu) / jnp.sqrt(var + EPS) * ln_gamma + ln_beta
        qkv = normed @ W_qkv.T
        q, k, v = jnp.split(qkv, 3, axis=-1)

        def to_heads(t):
            return t.reshape(B, N, H, D).transpose(0, 2, 1, 3)
        q, k, v = (to_heads(q), to_heads(k), to_heads(v))
        gate = jax.nn.sigmoid(to_heads(x @ W_gate.T + b_gate))
        scores = jnp.einsum('bhid,bhjd->bhij', q, k) * D ** (-0.5)
        attn = jax.nn.softmax(scores, axis=-1)
        out = jnp.einsum('bhij,bhid->bhjd', attn, v) * gate
        out = out.transpose(0, 2, 1, 3).reshape(B, N, H * D)
        return x + out @ W_final.T + b_final

    def _L0_ffn_ref(x, gate_w, gate_b, w1, b1, w2, b2, gamma, beta):
        import jax, jax.numpy as jnp
        import numpy as np
        B, S, H, F, E, K = (8, 1024, 64, 128, 16, 2)
        EPS = 1e-05
        gate_logits = x @ gate_w + gate_b
        topk_vals, topk_idx = jax.lax.top_k(gate_logits, K)
        topk_w = jax.nn.softmax(topk_vals, axis=-1)
        h = jax.nn.relu(jnp.einsum('bsh,ehf->bsef', x, w1) + b1)
        expert_out = jnp.einsum('bsef,efh->bseh', h, w2) + b2
        sel = jnp.take_along_axis(expert_out, topk_idx[:, :, :, None], axis=2)
        moe = jnp.sum(topk_w[..., None] * sel, axis=2)
        y = x + moe
        mu = jnp.mean(y, axis=-1, keepdims=True)
        var = jnp.var(y, axis=-1, keepdims=True)
        return (y - mu) / jnp.sqrt(var + EPS) * gamma + beta
    h = _L0_tok_ref(x, L0_tok_emb, L0_tok_W, L0_tok_b)
    h = h + _L0_attn_ref(_layernorm(h, axis=-1), L0_attn_ln_gamma, L0_attn_ln_beta, L0_attn_W_qkv, L0_attn_W_gate, L0_attn_b_gate, L0_attn_W_final, L0_attn_b_final)
    h = h + _L0_ffn_ref(_layernorm(h, axis=-1), L0_ffn_gate_w, L0_ffn_gate_b, L0_ffn_w1, L0_ffn_b1, L0_ffn_w2, L0_ffn_b2, L0_ffn_gamma, L0_ffn_beta)
    return h

_drawn_inputs = setup_inputs


def setup_inputs(seed=0):
    import zlib

    import numpy as np

    out = dict(_drawn_inputs(seed))
    spreads = {'L0_attn_ln_gamma': (1.0, 0.6),
     'L0_attn_ln_beta': (0.0, 0.8),
     'L0_attn_b_gate': (1.0, 0.6),
     'L0_attn_b_final': (0.0, 0.1),
     'L0_ffn_gate_b': (0.0, 0.1),
     'L0_ffn_b1': (0.0, 0.8),
     'L0_ffn_b2': (0.0, 0.294),
     'L0_ffn_gamma': (1.0, 0.2),
     'L0_ffn_beta': (0.0, 0.1)}
    factors = {'L0_attn_W_gate': 8.0, 'L0_ffn_w1': 7.53, 'L0_ffn_w2': 5.042}
    for name, (base, spread) in spreads.items():
        noise = np.random.default_rng([zlib.crc32(name.encode()), seed]).standard_normal(out[name].shape)
        drawn = base * np.exp(spread * noise) if base else spread * noise
        out[name] = jnp.asarray(drawn.astype(out[name].dtype))
    for name, factor in factors.items():
        out[name] = (out[name] * factor).astype(out[name].dtype)
    return out
```

```python
from contextlib import ExitStack

import concourse.bass as bass
from concourse import mybir

F32 = mybir.dt.float32
F32R = mybir.dt.float32r
I32 = mybir.dt.int32
ACT = mybir.ActivationFunctionType
ALU = mybir.AluOpType
X_AXIS = mybir.AxisListType.X

P = 128
BATCHES = 8
T = 512
NT = T // P
VOCAB = 50257
C = 64
TAPS = 9
WINDOW = TAPS * C
REACH = TAPS // 2
HEADS = 8
D = 32
GROUP = 4
GROUPS = HEADS // GROUP
INNER = HEADS * D
UNITS = GROUPS * NT
EXPERTS = 16
F = 128
EPS = 1e-5
SCALE = float(D) ** -0.5
BLOCKS = 5
EDGES = 2 * REACH
LOWER = -3e38
DMA = 16

USES = (
    [("attn", "v0"), ("attn", "v1"), ("moe", "project"), ("tok", "turn0"), ("tok", "turn1"), ("tok", "turn2")]
    + [("tok", "turn3"), ("tok", "turn4")]
    + [("moe", "turn_f"), ("tok", "conv"), ("tok", "rows")]
    + [("moe", "router"), ("attn", "gate0"), ("attn", "gate1")]
    + [("moe", "turn_c"), ("tok", "turn_n"), ("tok", "turn_a")]
    + [("tok", "q0"), ("tok", "k0"), ("moe", "e0"), ("moe", "e1")]
    + [("tok", "q1"), ("moe", "e2"), ("tok", "k1"), ("moe", "e3"), ("moe", "e4")]
    + [("moe", f"e{e}") for e in range(5, EXPERTS)]
    + [("moe", "sum")]
)
ALL = ("tok", "attn", "moe")


def uses_of(parts):
    return [name for part, name in USES if part in parts]


class Batch:

    def __init__(self, number, register=None):
        self.number, self.register = number, register

    def count(self, per, n=0):
        value = self.number * per + n
        return value if self.register is None else self.register * per + value

    def index(self):
        return self.number if self.register is None else self.register + self.number

    def first(self):
        return self.register is None and self.number == 0


class Iteration:

    def __init__(self, i, parts, base, register=None):
        self.parts, self.base, self.register = parts, base, register
        self.tok = Batch(i + 1, register) if "tok" in parts else None
        self.attn = Batch(i, register) if "attn" in parts else None
        self.moe = Batch(i - 1, register) if "moe" in parts else None
        self.last_tok = register is None and i + 1 == BATCHES - 1
        self.local = {name: n for n, name in enumerate(uses_of(parts))}

    def full(self, name):
        value = self.base + self.local[name] + 1
        return value if self.register is None else self.register * len(self.local) + value

    def slot(self, name):
        return (self.base + self.local[name]) % 2

    def drained(self, name):
        value = (self.base + self.local[name]) // 2 + 1
        return value if self.register is None else self.register * (len(self.local) // 2) + value


def plan():
    base, before, after = 0, [], []
    loop = None
    for i in range(-1, BATCHES + 1):
        parts = tuple(p for p, first, last in (("tok", -1, BATCHES - 2), ("attn", 0, BATCHES - 1), ("moe", 1, BATCHES))
                      if first <= i <= last)
        row = (i, parts, base)
        if i < 2:
            before.append(row)
        elif i <= BATCHES - 3:
            loop = loop or row
        else:
            after.append(row)
        base += len(uses_of(parts))
    assert loop[2] % 2 == 0 and len(uses_of(ALL)) % 2 == 0
    return before, loop, BATCHES - 4, after


def run_iterations(engine, body):
    before, loop, count, after = plan()
    for i, parts, base in before:
        body(Iteration(i, parts, base))
    i, parts, base = loop
    with engine.Fori(0, count) as j:
        body(Iteration(i, parts, base, j))
    for i, parts, base in after:
        body(Iteration(i, parts, base))


class Order:

    def __init__(self, sem, per):
        self.sem, self.per, self.n, self.batch = sem, per, 0, None

    def start(self, batch):
        self.n, self.batch = 0, batch

    def mark(self, instruction):
        instruction.then_inc(self.sem, 1)
        self.n += 1

    def value(self):
        assert self.n <= self.per
        return self.batch.count(self.per, self.n)

    def wait(self, engine):
        engine.wait_ge(self.sem, self.value())

    def end(self):
        assert self.n == self.per, (self.n, self.per)


def tower_kernel(nc, x, emb, conv_w, conv_b, ln_gamma, ln_beta, w_qkv, w_gate, b_gate, w_final, b_final,
                 router_w, router_b, w1, b1, w2, b2, gamma, beta, out):
    with ExitStack() as ctx:
        def sb(name, shape, dtype=F32):
            return ctx.enter_context(nc.sbuf_tensor(name, shape, dtype))

        def sem(name):
            return ctx.enter_context(nc.semaphore(name))

        ident = sb("ident", [P, P])
        halves = sb("halves", [P, C])
        wc = sb("wc", [P, BLOCKS, C])
        w_qkv_hi, w_qkv_lo = sb("w_qkv_hi", [P, 3 * INNER], F32R), sb("w_qkv_lo", [P, 3 * INNER], F32R)
        w_gate_hi, w_gate_lo = sb("w_gate_hi", [P, INNER], F32R), sb("w_gate_lo", [P, INNER], F32R)
        router_hi, router_lo = sb("router_hi", [P, EXPERTS], F32R), sb("router_lo", [P, EXPERTS], F32R)
        half_wf = sb("half_wf", [P, GROUPS, C])
        w1_hi = sb("w1_hi", [P, EXPERTS, F], F32R)
        BIAS_ROWS = 2
        w1_lo = sb("w1_lo", [C + BIAS_ROWS, EXPERTS, F], F32R)
        w2_sb = sb("w2_sb", [P, EXPERTS, C])
        b2_sb = sb("b2_sb", [EXPERTS, C])
        half_bg = sb("half_bg", [P, GROUPS])
        ln_g, ln_b, bf = sb("ln_g", [P, C]), sb("ln_b", [P, C]), sb("bf", [P, C])
        ffn_g, ffn_b, router_bias = sb("ffn_g", [P, C]), sb("ffn_b", [P, C]), sb("router_bias", [P, EXPERTS])
        minus_half = sb("minus_half", [P, 2 * NT])
        expert_ids = sb("expert_ids", [P, EXPERTS])
        edge_ids = sb("edge_ids", [P, 2])
        windows = sb("windows", [P, BATCHES * NT], I32)
        edge_t = sb("edge_t", [P, BLOCKS, EDGES])

        window_now = sb("window_now", [P, NT], I32)
        gathered_rows = sb("gathered_rows", [P, NT, WINDOW])
        turned = sb("turned", [P, BLOCKS, T])
        x_edge = sb("x_edge", [C + EDGES, T], I32)
        conv_t = sb("conv_t", [P, T])
        h0 = sb("h0", [P, NT, C])
        stats_k, mean_k = sb("stats_k", [P, NT, 6]), sb("mean_k", [P, NT, 2])
        var_k, rstd_k, inv_k = sb("var_k", [P, 2, NT]), sb("rstd_k", [P, 2, NT]), sb("inv_k", [P, NT])
        a_twice, n_twice = sb("a_twice", [P, NT, 2, C]), sb("n_twice", [P, NT, 2, C])
        n_hat = sb("n_hat", [P, NT, C])
        sum_next, sum_now = sb("sum_next", [P, NT, C]), sb("sum_now", [P, NT, C])
        n_split, a_split = sb("n_split", [P, T], F32R), sb("a_split", [P, T], F32R)
        qk_flat = sb("qk_flat", [P, GROUPS, 4, T], F32R)
        q_stack, k_stack = sb("q_stack", [P, HEADS, T], F32R), sb("k_stack", [P, HEADS, T], F32R)

        v_rows = sb("v_rows", [P, NT, INNER])
        gate = sb("gate", [P, GROUPS, T])
        neg_max, z, inv_z = sb("neg_max", [P, 2, GROUP]), sb("z", [P, 2, GROUP]), sb("inv_z", [P, 2, GROUP])
        probs = sb("probs", [P, 2, GROUP, T])
        v_scaled_sb = sb("v_scaled_sb", [P, 2, GROUP, D])
        gated = sb("gated", [P, GROUPS, T])

        h1 = sb("h1", [P, NT, C])
        stats_m, mean_m = sb("stats_m", [P, NT, 6]), sb("mean_m", [P, NT, 2])
        var_m, rstd_m = sb("var_m", [P, NT]), sb("rstd_m", [P, NT])
        f_twice = sb("f_twice", [P, NT, 2, C])
        f_split = sb("f_split", [P, T], F32R)
        f_ones = sb("f_ones", [C + BIAS_ROWS, T], F32R)
        logits, logits2 = sb("logits", [P, NT, EXPERTS]), sb("logits2", [P, NT, EXPERTS])
        same, cand = sb("same", [P, NT, EXPERTS]), sb("cand", [P, NT, EXPERTS])
        first_hot, second_hot = sb("first_hot", [P, NT, EXPERTS]), sb("second_hot", [P, NT, EXPERTS])
        top1, top2, which = sb("top1", [P, NT]), sb("top2", [P, NT]), sb("which", [P, NT])
        gap, e_gap, den, wt1, wt2 = (sb(n, [P, NT]) for n in ("gap", "e_gap", "den", "wt1", "wt2"))
        share = sb("share", [P, NT, EXPERTS])
        share_t = sb("share_t", [EXPERTS, T])
        QUARTER = EXPERTS // 4
        share_row = sb("share_row", [P, QUARTER, T])
        share_all = sb("share_all", [P, EXPERTS, T])
        hidden = sb("hidden", [P, 3, T])
        moe_t = sb("moe_t", [P, T])
        y_rows, y_hat, result = (sb(n, [P, NT, C]) for n in ("y_rows", "y_hat", "result"))

        scratch = nc.dram_tensor("scratch", (GROUPS, 2, 2, D, GROUP, T), F32).ap()

        scores = ctx.enter_context(nc.psum_tensor("scores", [P, GROUP, T], F32))
        attended = ctx.enter_context(nc.psum_tensor("attended", [P, T], F32))
        experts_sum = ctx.enter_context(nc.psum_tensor("experts_sum", [P, T], F32))
        shared = ctx.enter_context(nc.psum_tensor("shared", [P, 2, T], F32))

        weights_in, edges_in, x_in = sem("weights_in"), sem("edges_in"), sem("x_in")
        bias_rows_in = sem("bias_rows_in")
        consts_made, weights_made, bias_parts = sem("consts_made"), sem("weights_made"), sem("bias_parts")
        windows_made, edge_diff, edge_turned, edge_turned_in, edge_conv = (
            sem(n) for n in ("windows_made", "edge_diff", "edge_turned", "edge_turned_in", "edge_conv"))
        bank_full = sem("bank_full")
        bank_drained = [sem("bank_drained0"), sem("bank_drained1")]
        window_copied = sem("window_copied")
        rows_gathered = sem("rows_gathered")
        x_edge_in = sem("x_edge_in")
        edges_marked = sem("edges_marked")
        var_k_ready, rstd_k_ready = sem("var_k_ready"), sem("rstd_k_ready")
        a_ready, n_ready = sem("a_ready"), sem("n_ready")
        high_k = sem("high_k")
        scratch_in = [sem("scratch_in0"), sem("scratch_in1")]
        stack_in = [sem("stack_in0"), sem("stack_in1")]
        scores_ready, max_ready, probs_ready = sem("scores_ready"), sem("max_ready"), sem("probs_ready")
        v_scaled, unit_summed = sem("v_scaled"), sem("unit_summed")
        gated_ready = sem("gated_ready")
        sum_made, sum_copied = sem("sum_made"), sem("sum_copied")
        var_f_ready, rstd_f_ready = sem("var_f_ready"), sem("rstd_f_ready")
        f_ready, high_f = sem("f_ready"), sem("high_f")
        gap_ready, e_gap_ready, share_ready = sem("gap_ready"), sem("e_gap_ready"), sem("share_ready")
        share_row_in, share_spread = sem("share_row_in"), sem("share_spread")
        experts_summed, moe_t_ready = sem("experts_summed"), sem("moe_t_ready")
        var_y_ready, rstd_y_ready, y_ready = sem("var_y_ready"), sem("rstd_y_ready"), sem("y_ready")
        result_ready, stored = sem("result_ready"), sem("stored")
        vector_setup, pool_setup = Order(sem("vector_setup"), 99), Order(sem("pool_setup"), 99)
        vector_attn = Order(sem("vector_attn"), UNITS)
        vector_tok = Order(sem("vector_tok"), 15)
        vector_moe = Order(sem("vector_moe"), 38)
        pool_tok = Order(sem("pool_tok"), 3)
        pool_moe = Order(sem("pool_moe"), 2)

        stage = share_all[:].rearrange("p e t -> p (e t)")
        offset = [0]

        def staged(rows, n):
            view = stage[0:rows, offset[0]:offset[0] + n]
            offset[0] += n
            return view

        raw_qkv, raw_gate, raw_router, raw_w1 = staged(P, 3 * INNER), staged(P, INNER), staged(P, EXPERTS), staged(P, EXPERTS * F)
        raw_b1 = staged(1, EXPERTS * F)
        b1_hi, b1_lo = staged(1, EXPERTS * F).bitcast(F32R), raw_b1.bitcast(F32R)

        edge_a, edge_b = (probs[0:EDGES, n, 0:2, :].rearrange("e h t -> e (h t)")[:, 0:WINDOW].rearrange("e (k c) -> e k c", c=C)
                          for n in range(2))

        WEIGHT_LOADS = 22
        block = ctx.enter_context(nc.Block())

        def bank(it, name):
            return shared[:, it.slot(name), :]

        def drained(engine, it, name):
            engine.wait_ge(bank_drained[it.slot(name)], it.drained(name))

        def in_register(engine, value):
            return value if isinstance(value, int) else engine.snap(engine.to_reg(value))

        def wait_apart(engine, semaphore, value):
            value = in_register(engine, value)
            engine.wait_ge(consts_made, 1)
            engine.wait_ge(semaphore, value)

        def both_halves(dst, src):
            return [(dst[0:C], src), (dst[C:P], src)]

        @block.sync
        def _(sp):
            sp.dma_start(windows[:].rearrange("p (b t) -> p b t", b=BATCHES),
                         x.rearrange("b (p t) -> p b t", t=NT)).then_inc(x_in, DMA)
            for lo in range(0, EDGES, REACH):
                start = 0 if lo == 0 else VOCAB - TAPS
                sp.dma_start(edge_b[lo:lo + REACH].rearrange("e k c -> e (k c)"),
                             emb[start:start + TAPS, :].rearrange("k c -> (k c)")[None, :].to_broadcast([REACH, WINDOW])
                             ).then_inc(edges_in, DMA)
            for e in range(EDGES):
                token = e if e < REACH else VOCAB - EDGES + e
                first, last = token - REACH, token + REACH
                below, above = max(0, -first), max(0, last - (VOCAB - 1))
                sp.dma_start(edge_a[e:e + 1, below:TAPS - above, :],
                             emb[first + below:last - above + 1, :][None]).then_inc(edges_in, DMA)
                at, row, n = (0, 0, below) if below else (TAPS - above, VOCAB - 1, above)
                sp.dma_start(edge_a[e:e + 1, at:at + n, :],
                             emb[row:row + 1, :][None].to_broadcast([1, n, C])).then_inc(edges_in, DMA)
            sp.wait_ge(bias_parts, 2)
            for n, part in enumerate((b1_hi, b1_lo)):
                sp.dma_start(w1_lo[C + n:C + n + 1].rearrange("p e f -> p (e f)").bitcast(F32),
                             part.bitcast(F32)).then_inc(bias_rows_in, DMA)

            def load_x_edge(k):
                if not k.first():
                    sp.wait_ge(edges_marked, k.count(1))
                row = x[k.number:k.number + 1, :] if k.register is None else x[bass.ds(k.index(), 1), :]
                sp.dma_start(x_edge[C:C + EDGES, :], row.to_broadcast([EDGES, T])).then_inc(x_edge_in, DMA)

            def stack(it, g):
                k = it.tok
                for name in (f"q{g}", f"k{g}"):
                    wait_apart(sp, bank_drained[it.slot(name)], it.drained(name))
                if not k.first():
                    sp.wait_ge(stack_in[g], k.count(5 * DMA))
                for side in range(2):
                    for part in range(2):
                        sp.dma_start(scratch[g, side, part].rearrange("d h n -> h d n"),
                                     qk_flat[:, g, 2 * side + part, :].bitcast(F32)).then_inc(scratch_in[g], DMA)
                if not k.first():
                    scored = in_register(sp, Batch(k.number - 1, k.register).count(2 * UNITS, 2 * NT * (g + 1)))
                sp.wait_ge(scratch_in[g], k.count(4 * DMA, 4 * DMA))
                if not k.first():
                    sp.wait_ge(scores_ready, scored)
                heads = slice(GROUP * g, GROUP * (g + 1))
                for lo in (0, 2 * D):
                    sp.dma_start(q_stack[lo:lo + 2 * D, heads, :].bitcast(F32),
                                 scratch[g, 0].rearrange("s d h n -> (s d) h n")).then_inc(stack_in[g], DMA)
                sp.dma_start(k_stack[0:2 * D, heads, :].bitcast(F32),
                             scratch[g, 1].rearrange("s d h n -> (s d) h n")).then_inc(stack_in[g], DMA)
                sp.dma_start(k_stack[2 * D:3 * D, heads, :].bitcast(F32), scratch[g, 1, 1]).then_inc(stack_in[g], DMA)
                sp.dma_start(k_stack[3 * D:4 * D, heads, :].bitcast(F32), scratch[g, 1, 0]).then_inc(stack_in[g], DMA)

            def iteration(it):
                if it.tok:
                    load_x_edge(it.tok)
                if it.moe:
                    m = it.moe
                    wait_apart(sp, bank_drained[it.slot("turn_c")], it.drained("turn_c"))
                    if not m.first():
                        sp.wait_ge(share_spread, m.count(4))
                    for g in range(4):
                        sp.dma_start(share_row[32 * g:32 * g + 1, :, :],
                                     share_t[QUARTER * g:QUARTER * (g + 1), :]).then_inc(share_row_in, DMA)
                if it.tok:
                    for g in range(GROUPS):
                        stack(it, g)
                if it.moe:
                    m = it.moe
                    sp.wait_ge(result_ready, m.count(1, 1))
                    rows = out[m.number] if m.register is None else out[bass.ds(m.index(), 1)].rearrange("a n c -> (a n) c")
                    sp.dma_start(rows.rearrange("(p t) c -> p (t c)", t=NT),
                                 result[:].rearrange("p t c -> p (t c)")).then_inc(stored, DMA)

            run_iterations(sp, iteration)
            sp.wait_ge(stored, DMA * BATCHES)

        @block.gpsimd
        def _(pool):
            pool_setup.start(Batch(0))
            pool_setup.mark(pool.memset(ident[:], 0.0))
            pool_setup.mark(pool.iota(edge_ids[:, 0:1].bitcast(I32), pattern=[[0, 1]], base=-C, channel_multiplier=1))
            pool_setup.mark(pool.iota(expert_ids[:].bitcast(I32), pattern=[[1, EXPERTS]], base=-EXPERTS, channel_multiplier=0))
            pool_setup.mark(pool.memset(minus_half[:], -0.5))
            pool_setup.wait(pool)
            pool.affine_select(out=ident[:], in_=ident[:], compare_op=ALU.not_equal, fill=1.0, base=0,
                               pattern=[[-1, P]], channel_multiplier=1).then_inc(consts_made, 1)

            def gather(k):
                if not k.first():
                    wait_apart(pool, rows_gathered, k.count(NT * DMA))
                else:
                    pool.wait_ge(windows_made, 1)
                start = k.index() * NT
                cols = windows[:, start:start + NT] if k.register is None else windows[:, bass.ds(start, NT)]
                pool.tensor_copy(window_now[:], cols).then_inc(window_copied, 1)
                wait_apart(pool, window_copied, k.count(1, 1))
                for t in range(NT):
                    pool.indirect_dma_start(
                        out=gathered_rows[:, t, :], out_offset=None, in_=emb,
                        in_offset=bass.IndirectOffsetOnAxis(ap=window_now[:, t:t + 1], axis=0),
                    ).then_inc(rows_gathered, DMA)

            gather(Batch(0))

            def iteration(it):
                a, k, m = it.attn, it.tok, it.moe
                if a:
                    if m:
                        drained(pool, it, "project")
                    wait_apart(pool, n_ready, a.count(1, 1))
                    pool.tensor_copy(sum_now[:], sum_next[:]).then_inc(sum_copied, 1)
                if m:
                    pool_moe.start(m)
                    wait_apart(pool, var_f_ready, m.count(1, 1))
                    pool.tensor_tensor(rstd_m[:], var_m[:], minus_half[:, 0:NT], ALU.pow).then_inc(rstd_f_ready, 1)
                if k:
                    pool_tok.start(k)
                    if not it.last_tok:
                        pool.wait_ge(bank_full, it.full("turn4"))
                        gather(Batch(k.number + 1, k.register))
                    wait_apart(pool, var_k_ready, k.count(1, 1))
                    pool.tensor_tensor(rstd_k[:].rearrange("p a t -> p (a t)"), var_k[:].rearrange("p a t -> p (a t)"),
                                       minus_half[:], ALU.pow).then_inc(rstd_k_ready, 1)
                    pool.wait_ge(a_ready, k.count(1, 1))
                    pool.wait_ge(rstd_k_ready, k.count(1, 1))
                    pool_tok.mark(pool.tensor_tensor(n_hat[:], a_twice[:, :, 0, :],
                                                     rstd_k[:, 1, :, None].to_broadcast([P, NT, C]), ALU.mult))
                    if not k.first():
                        pool.wait_ge(sum_copied, k.count(1))
                    pool_tok.mark(pool.tensor_tensor(sum_next[:], h0[:], a_twice[:, :, 0, :], ALU.add))
                    pool_tok.wait(pool)
                    pool_tok.mark(pool.tensor_tensor(n_hat[:], n_hat[:], ln_g[:, None, :].to_broadcast([P, NT, C]), ALU.mult))
                    pool_tok.wait(pool)
                    pool_tok.end()
                    pool.tensor_tensor(sum_next[:], sum_next[:], bf[:, None, :].to_broadcast([P, NT, C]), ALU.add
                                       ).then_inc(sum_made, 1)
                    pool.tensor_tensor(n_twice[:], n_hat[:, :, None, :].to_broadcast([P, NT, 2, C]),
                                       ln_b[:, None, None, :].to_broadcast([P, NT, 2, C]), ALU.add).then_inc(n_ready, 1)
                if m:
                    for g in range(4):
                        if g == 0:
                            if k and not it.last_tok:
                                pool.wait_ge(rows_gathered, k.count(NT * DMA, 2 * NT * DMA))
                            if not m.first():
                                pool.wait_ge(moe_t_ready, m.count(1))
                            wait_apart(pool, share_row_in, m.count(4 * DMA, 4 * DMA))
                        else:
                            wait_apart(pool, share_spread, m.count(4, g))
                        pool.partition_broadcast(share_all[:, QUARTER * g:QUARTER * (g + 1), :].rearrange("p e t -> p (e t)"),
                                                 share_row[32 * g:32 * g + 1, :, :].rearrange("p e t -> p (e t)")
                                                 ).then_inc(share_spread, 1)
                    statistics_made = in_register(pool, m.count(1, 1))
                    wait_apart(pool, share_spread, m.count(4, 4))
                    pool.wait_ge(var_y_ready, statistics_made)
                    pool.tensor_tensor(rstd_m[:], var_m[:], minus_half[:, 0:NT], ALU.pow).then_inc(rstd_y_ready, 1)
                    pool.wait_ge(y_ready, m.count(1, 1))
                    pool_moe.mark(pool.tensor_tensor(y_hat[:], y_hat[:], ffn_g[:, None, :].to_broadcast([P, NT, C]), ALU.mult))
                    pool_moe.wait(pool)
                    pool_moe.mark(pool.tensor_tensor(y_hat[:], y_hat[:], ffn_b[:, None, :].to_broadcast([P, NT, C]), ALU.add))
                    pool_moe.wait(pool)
                    pool_moe.end()
                    if not m.first():
                        pool.wait_ge(stored, m.count(DMA))
                    pool.tensor_tensor(result[:], y_hat[:], h1[:], ALU.add).then_inc(result_ready, 1)

            run_iterations(pool, iteration)

        @block.scalar
        def _(act):
            loads = (
                [(wc[:, 0:4, :], conv_w[0:4 * P, :].rearrange("(b p) o -> p b o", p=P)),
                 (wc[0:C, 4, :], conv_w[4 * P:WINDOW, :]), (wc[C + EDGES:C + EDGES + 1, 4, :], conv_b)]
                + both_halves(raw_qkv, w_qkv) + both_halves(raw_gate, w_gate) + both_halves(raw_router, router_w)
                + both_halves(raw_w1, w1) + [(raw_b1, b1)]
                + [(half_wf[:], w_final.rearrange("(g p) o -> p g o", p=P)), (half_bg[:], b_gate)]
                + [(w2_sb[:].rearrange("p e o -> p (e o)"), w2), (b2_sb[:], b2)]
                + [(dst[:], src.to_broadcast([P, src.shape[1]]))
                   for dst, src in ((ln_g, ln_gamma), (ln_b, ln_beta), (bf, b_final), (ffn_g, gamma), (ffn_b, beta),
                                    (router_bias, router_b))]
            )
            assert len(loads) == WEIGHT_LOADS, len(loads)
            for dst, src in loads:
                act.dma_start(dst, src).then_inc(weights_in, DMA)

            def copy_out(it, name, dst, src):
                act.wait_ge(bank_full, it.full(name))
                nc.scalar.activation(dst, src, ACT.Copy).then_inc(bank_drained[it.slot(name)], 1)

            def exponentials(b, u, pair):
                act.wait_ge(max_ready, b.count(2 * UNITS, 2 * u + pair + 1))
                if u >= 2 or not b.first():
                    act.wait_ge(unit_summed, b.count(UNITS, u - 1))
                for j in range(2 * pair, 2 * pair + 2):
                    last = nc.scalar.activation(probs[:, u % 2, j, :], scores[:, j, :], ACT.Exp,
                                                bias=neg_max[:, u % 2, j:j + 1], accum_out=z[:, u % 2, j:j + 1])
                last.then_inc(probs_ready, 1)

            def high_part(it, name, dst, scale=1.0):
                act.wait_ge(bank_full, it.full(name))
                return nc.scalar.activation(dst, bank(it, name), ACT.Copy, scale=scale)

            def iteration(it):
                a, k, m = it.attn, it.tok, it.moe
                for u in range(UNITS):
                    if a:
                        exponentials(a, u, 0)
                    if u == 0 and a:
                        if not a.first():
                            act.wait_ge(v_scaled, a.count(UNITS))
                        for n in range(2):
                            copy_out(it, f"v{n}", v_rows[:, 2 * n:2 * n + 2, :].rearrange("p t c -> p (t c)"), bank(it, f"v{n}"))
                    if u == 2 and m:
                        high_part(it, "turn_f", f_split[:])
                        nc.scalar.activation(f_ones[0:C, :], bank(it, "turn_f")[0:C, :], ACT.Copy).then_inc(high_f, 1)
                    if u == 2 and k:
                        copy_out(it, "conv", conv_t[:], bank(it, "conv"))
                    if u == 4 and m:
                        if not m.first():
                            act.wait_ge(share_row_in, m.count(4 * DMA))
                        copy_out(it, "turn_c", share_t[:], bank(it, "turn_c")[0:EXPERTS, :])
                    if u == 4 and k:
                        high_part(it, "turn_n", n_split[:]).then_inc(high_k, 1)
                    if u in (5, 6) and k:
                        g = u - 5
                        if not k.first():
                            act.wait_ge(scratch_in[g], k.count(4 * DMA))
                        high_part(it, f"q{g}", qk_flat[:, g, 0, :], SCALE).then_inc(high_k, 1)
                    if a:
                        exponentials(a, u, 1)
                    if u == 0 and k:
                        for n in range(3):
                            copy_out(it, f"turn{n}", turned[:, n, :], bank(it, f"turn{n}"))
                    if u == 1 and k:
                        copy_out(it, "turn3", turned[:, 3, :], bank(it, "turn3"))
                        copy_out(it, "turn4", turned[0:C, 4, :], bank(it, "turn4")[0:C, :])
                    if u == 2 and k:
                        if not k.first():
                            act.wait_ge(sum_made, k.count(1))
                        copy_out(it, "rows", h0[:].rearrange("p t c -> p (t c)"), bank(it, "rows")[:, 0:NT * C])
                    if u == 3 and a:
                        if not a.first():
                            act.wait_ge(gated_ready, a.count(GROUPS))
                        for g in range(GROUPS):
                            act.wait_ge(bank_full, it.full(f"gate{g}"))
                            nc.scalar.activation(gate[:, g, :], bank(it, f"gate{g}"), ACT.Tanh, bias=half_bg[:, g:g + 1],
                                                 scale=0.5).then_inc(bank_drained[it.slot(f"gate{g}")], 1)
                    if u == 3 and m:
                        act.wait_ge(gap_ready, m.count(1, 1))
                        nc.scalar.activation(e_gap[:], gap[:], ACT.Exp).then_inc(e_gap_ready, 1)
                    if u == 4 and k:
                        high_part(it, "turn_a", a_split[:]).then_inc(high_k, 1)
                    if u in (5, 6) and k:
                        high_part(it, f"k{u - 5}", qk_flat[:, u - 5, 2, :]).then_inc(high_k, 1)
                if m:
                    act.wait_ge(experts_summed, m.count(1, 1))
                    nc.scalar.activation(moe_t[:], experts_sum[:], ACT.Copy).then_inc(moe_t_ready, 1)

            act.wait_ge(weights_made, 1)
            run_iterations(act, iteration)

        @block.vector
        def _(dve):
            vector_setup.start(Batch(0))
            mark = vector_setup.mark

            def wait():
                vector_setup.wait(dve)

            mark(dve.memset(turned[C:P, BLOCKS - 1, :], 1.0))
            mark(dve.memset(f_ones[C:C + BIAS_ROWS, :].bitcast(F32), 1.0))
            dve.wait_ge(x_in, DMA)
            mark(dve.tensor_scalar(windows[:], windows[:], REACH, 0, ALU.subtract, ALU.max))
            wait()
            dve.tensor_scalar(windows[:], windows[:], VOCAB - TAPS, None, ALU.min).then_inc(windows_made, 1)
            dve.wait_ge(consts_made, 1)
            ids = edge_ids[:, 0:1]
            mark(dve.tensor_copy(edge_ids[:, 1:2], ids.bitcast(I32)))
            mark(dve.tensor_copy(same[:, 0, :], expert_ids[:].bitcast(I32)))
            wait()
            mark(dve.tensor_copy(expert_ids[:], same[:, 0, :]))
            mark(dve.tensor_scalar(ids, edge_ids[:, 1:2], REACH - 0.5, VOCAB - EDGES, ALU.is_ge, ALU.mult))
            wait()
            mark(dve.tensor_tensor(ids, ids, edge_ids[:, 1:2], ALU.add))
            mark(dve.tensor_tensor(halves[:], ident[:, 0:C], ident[:, C:P], ALU.add))
            dve.wait_ge(edges_in, (2 + 2 * EDGES) * DMA)
            dve.tensor_tensor(edge_a, edge_a, edge_b, ALU.subtract).then_inc(edge_diff, 1)
            dve.wait_ge(weights_in, WEIGHT_LOADS * DMA)
            dve.tensor_copy(b1_hi, raw_b1).then_inc(bias_parts, 1)
            pairs = ((w_qkv_hi[:], w_qkv_lo[:], raw_qkv), (w_gate_hi[:], w_gate_lo[:], raw_gate),
                     (router_hi[:], router_lo[:], raw_router),
                     (w1_hi[:].rearrange("p e f -> p (e f)"), w1_lo[0:C].rearrange("p e f -> p (e f)"), raw_w1))
            for hi, lo, raw in pairs:
                mark(dve.tensor_copy(hi, raw))
            wait()
            dve.wait_ge(bias_parts, 1)
            dve.tensor_tensor(b1_lo, raw_b1, b1_hi, ALU.subtract).then_inc(bias_parts, 1)
            for hi, lo, raw in pairs:
                rows = lo.shape[0]
                mark(dve.tensor_tensor(lo, raw[0:rows], hi[0:rows], ALU.subtract))
            mark(dve.tensor_scalar(half_wf[:], half_wf[:], 0.5, None, ALU.mult))
            mark(dve.tensor_scalar(half_bg[:], half_bg[:], 0.5, None, ALU.mult))
            wait()
            dve.wait_ge(edge_turned, 1)
            full = BLOCKS - 1
            dve.tensor_copy(edge_t[:, 0:full, :], attended[:, 0:full * EDGES].rearrange("p (k e) -> p k e", e=EDGES)
                            ).then_inc(edge_turned_in, 1)
            dve.tensor_copy(edge_t[0:C, full, :], attended[0:C, full * EDGES:BLOCKS * EDGES]).then_inc(edge_turned_in, 1)
            dve.wait_ge(edge_conv, 1)
            dve.tensor_copy(wc[C:C + EDGES, 4, :], experts_sum[C:C + EDGES, 0:C]).then_inc(weights_made, 1)

            def maxima(b, u, pair):
                dve.wait_ge(scores_ready, b.count(2 * UNITS, 2 * u + pair + 1))
                dve.tensor_reduce(neg_max[:, u % 2, 2 * pair:2 * pair + 2], scores[:, 2 * pair:2 * pair + 2, :], X_AXIS,
                                  ALU.max, negate=True).then_inc(max_ready, 1)

            def scale_values(it, u):
                b = it.attn
                dve.wait_ge(probs_ready, b.count(2 * UNITS, 2 * u + 2))
                if u >= 2 or not b.first():
                    dve.wait_ge(unit_summed, b.count(UNITS, u - 1))
                vector_attn.mark(dve.reciprocal(inv_z[:, u % 2, :], z[:, u % 2, :]))
                if u == 0:
                    drained(dve, it, "v0")
                    drained(dve, it, "v1")
                vector_attn.wait(dve)
                g, t = divmod(u, NT)
                dve.tensor_tensor(v_scaled_sb[:, u % 2], v_rows[:, t, g * P:(g + 1) * P].rearrange("p (h d) -> p h d", d=D),
                                  inv_z[:, u % 2, :, None].to_broadcast([P, GROUP, D]), ALU.mult).then_inc(v_scaled, 1)

            def apply_gate(it, g):
                b = it.attn
                dve.wait_ge(unit_summed, b.count(UNITS, NT * (g + 1)))
                drained(dve, it, f"gate{g}")
                dve.scalar_tensor_tensor(gated[:, g, :], gate[:, g, :], 1.0, attended[:], ALU.add, ALU.mult
                                         ).then_inc(gated_ready, 1)

            def statistics(order, src, stats, mean):
                for t in range(NT):
                    order.mark(dve.bn_stats(stats[:, t, :], src[:, t, :]))
                wait_apart(dve, order.sem, order.value())
                for t in range(NT):
                    order.mark(dve.bn_aggr(mean[:, t, :], stats[:, t, :]))
                order.wait(dve)

            def normalise(dst, src, mean, rstd):
                for t in range(NT):
                    last = dve.tensor_scalar(dst(t), src(t), mean[:, t, 0:1], rstd(t), ALU.subtract, ALU.mult)
                    yield last

            def twice(tile, t):
                return tile[:, t, None, :].to_broadcast([P, 2, C])

            def low_part(it, name, dst, high, scale=None):
                src = bank(it, name)[C:P, :] if scale is None else bank(it, name)
                if scale is None or scale == 1.0:
                    ins = dve.tensor_tensor(dst, src, high, ALU.subtract)
                else:
                    ins = dve.scalar_tensor_tensor(dst, src, scale, high, ALU.mult, ALU.subtract)
                ins.then_inc(bank_drained[it.slot(name)], 1)

            def mark_edges(k):
                dve.wait_ge(x_edge_in, k.count(DMA, DMA))
                if not k.first():
                    dve.wait_ge(rstd_k_ready, k.count(1))
                dve.tensor_scalar(turned[C:C + EDGES, 4, :].rearrange("e (t p) -> e p t", t=NT),
                                  x_edge[C:C + EDGES, :].rearrange("e (p t) -> e p t", t=NT),
                                  edge_ids[C:C + EDGES, 0:1], None, ALU.is_equal).then_inc(edges_marked, 1)

            def norms_k(it):
                k = it.tok
                o = vector_tok
                o.start(k)
                drained(dve, it, "rows")
                statistics(o, h0, stats_k, mean_k)
                var = mean_k[:, :, 1]
                o.mark(dve.tensor_scalar(var_k[:, 0, :], var, EPS, None, ALU.add))
                o.wait(dve)
                o.mark(dve.reciprocal(inv_k[:], var_k[:, 0, :]))
                o.wait(dve)
                o.mark(dve.tensor_tensor(inv_k[:], inv_k[:], var, ALU.mult))
                o.wait(dve)
                dve.tensor_scalar(var_k[:, 1, :], inv_k[:], EPS, None, ALU.add).then_inc(var_k_ready, 1)
                dve.wait_ge(rstd_k_ready, k.count(1, 1))
                if not k.first():
                    dve.wait_ge(sum_made, k.count(1))
                ins = list(normalise(lambda t: a_twice[:, t], lambda t: twice(h0, t), mean_k, lambda t: rstd_k[:, 0, t:t + 1]))
                for one in ins[:-1]:
                    o.mark(one)
                ins[-1].then_inc(a_ready, 1)
                o.wait(dve)
                o.mark(dve.tensor_copy(inv_k[:, 0:1], var_k[:, 1, 0:1]))
                o.end()

            def norm_f_statistics(it):
                m = it.moe
                o = vector_moe
                o.start(m)
                dve.wait_ge(bank_full, it.full("project"))
                dve.wait_ge(sum_copied, m.count(1, 1))
                if not m.first():
                    dve.wait_ge(result_ready, m.count(1))
                dve.tensor_tensor(h1[:].rearrange("p t c -> p (t c)"), bank(it, "project")[:, 0:NT * C],
                                  sum_now[:].rearrange("p t c -> p (t c)"), ALU.add).then_inc(bank_drained[it.slot("project")], 1)
                drained(dve, it, "project")
                statistics(o, h1, stats_m, mean_m)
                dve.tensor_scalar(var_m[:], mean_m[:, :, 1], EPS, None, ALU.add).then_inc(var_f_ready, 1)

            def norm_f(it):
                m = it.moe
                dve.wait_ge(rstd_f_ready, m.count(1, 1))
                ins = list(normalise(lambda t: f_twice[:, t], lambda t: twice(h1, t), mean_m, lambda t: rstd_m[:, t:t + 1]))
                for one in ins[:-1]:
                    vector_moe.mark(one)
                ins[-1].then_inc(f_ready, 1)

            wide = [P, NT, EXPERTS]

            def best_two(it):
                m = it.moe
                o = vector_moe
                dve.wait_ge(bank_full, it.full("router"))
                dve.tensor_tensor(logits[:], bank(it, "router")[:, 0:NT * EXPERTS].rearrange("p (t e) -> p t e", e=EXPERTS),
                                  router_bias[:, None, :].to_broadcast(wide), ALU.add).then_inc(bank_drained[it.slot("router")], 1)
                drained(dve, it, "router")

                def best(src, top, hot):
                    o.mark(dve.tensor_reduce(top[:], src[:], X_AXIS, ALU.max))
                    o.wait(dve)
                    o.mark(dve.tensor_tensor(same[:], src[:], top[:, :, None].to_broadcast(wide), ALU.is_equal))
                    o.wait(dve)
                    o.mark(dve.tensor_tensor(cand[:], same[:], expert_ids[:, None, :].to_broadcast(wide), ALU.mult))
                    o.wait(dve)
                    o.mark(dve.tensor_reduce(which[:], cand[:], X_AXIS, ALU.min))
                    o.wait(dve)
                    o.mark(dve.tensor_tensor(hot[:], expert_ids[:, None, :].to_broadcast(wide),
                                             which[:, :, None].to_broadcast(wide), ALU.is_equal))
                    o.wait(dve)

                best(logits, top1, first_hot)
                o.mark(dve.scalar_tensor_tensor(logits2[:], first_hot[:], LOWER, logits[:], ALU.mult, ALU.add))
                o.wait(dve)
                best(logits2, top2, second_hot)
                dve.tensor_tensor(gap[:], top2[:], top1[:], ALU.subtract).then_inc(gap_ready, 1)

            def share_out(it):
                m, o = it.moe, vector_moe
                dve.wait_ge(e_gap_ready, m.count(1, 1))
                o.mark(dve.tensor_scalar(den[:], e_gap[:], 1.0, None, ALU.add))
                o.wait(dve)
                o.mark(dve.reciprocal(wt1[:], den[:]))
                o.wait(dve)
                o.mark(dve.tensor_tensor(wt2[:], e_gap[:], wt1[:], ALU.mult))
                o.mark(dve.tensor_tensor(same[:], first_hot[:], wt1[:, :, None].to_broadcast(wide), ALU.mult))
                o.wait(dve)
                o.mark(dve.tensor_tensor(cand[:], second_hot[:], wt2[:, :, None].to_broadcast(wide), ALU.mult))
                o.wait(dve)
                dve.tensor_tensor(share[:], same[:], cand[:], ALU.add).then_inc(share_ready, 1)

            def expert(it, e):
                m = it.moe
                dve.wait_ge(bank_full, it.full(f"e{e}"))
                if e % QUARTER == 0:
                    dve.wait_ge(share_spread, m.count(4, e // QUARTER + 1))
                dve.scalar_tensor_tensor(hidden[:, e % 3, :], bank(it, f"e{e}"), 0.0, share_all[:, e, :], ALU.max, ALU.mult
                                         ).then_inc(bank_drained[it.slot(f"e{e}")], 1)

            def final_norm(it):
                m = it.moe
                o = vector_moe
                dve.wait_ge(bank_full, it.full("sum"))
                dve.tensor_tensor(y_rows[:], bank(it, "sum")[:, 0:NT * C].rearrange("p (t c) -> p t c", c=C),
                                  f_twice[:, :, 0, :], ALU.add).then_inc(bank_drained[it.slot("sum")], 1)
                drained(dve, it, "sum")
                statistics(o, y_rows, stats_m, mean_m)
                dve.tensor_scalar(var_m[:], mean_m[:, :, 1], EPS, None, ALU.add).then_inc(var_y_ready, 1)
                dve.wait_ge(rstd_y_ready, m.count(1, 1))
                ins = list(normalise(lambda t: y_hat[:, t, :], lambda t: y_rows[:, t, :], mean_m, lambda t: rstd_m[:, t:t + 1]))
                for one in ins[:-1]:
                    o.mark(one)
                ins[-1].then_inc(y_ready, 1)
                o.wait(dve)

            def iteration(it):
                a, k, m = it.attn, it.tok, it.moe
                if a:
                    vector_attn.start(a)
                for u in range(UNITS):
                    if a:
                        maxima(a, u, 0)
                        if u > 0:
                            scale_values(it, u - 1)
                        if u == NT + 1:
                            apply_gate(it, 0)
                    if u == 0 and k:
                        mark_edges(k)
                    if u == 0 and m:
                        norm_f_statistics(it)
                    if u == 2 and m:
                        dve.wait_ge(high_f, m.count(1, 1))
                        low_part(it, "turn_f", f_split[C:P, :], f_split[C:P, :])
                    if u == 4 and k:
                        dve.wait_ge(high_k, k.count(6, 1))
                        low_part(it, "turn_n", n_split[C:P, :], n_split[C:P, :])
                    if u in (5, 6) and k:
                        dve.wait_ge(high_k, k.count(6, 3 + 2 * (u - 5)))
                        low_part(it, f"q{u - 5}", qk_flat[:, u - 5, 1, :], qk_flat[:, u - 5, 0, :], SCALE)
                    if u == 6 and m:
                        expert(it, 2)
                    if u == 7 and m:
                        for e in (5, 6):
                            expert(it, e)
                    if a:
                        maxima(a, u, 1)
                    if u == 0 and m:
                        norm_f(it)
                    if u == 3 and m:
                        best_two(it)
                    if u == 3 and k:
                        norms_k(it)
                    if u == 3 and m:
                        share_out(it)
                    if u == 4 and k:
                        dve.wait_ge(high_k, k.count(6, 2))
                        low_part(it, "turn_a", a_split[C:P, :], a_split[C:P, :])
                    if u in (5, 6) and k:
                        dve.wait_ge(high_k, k.count(6, 4 + 2 * (u - 5)))
                        low_part(it, f"k{u - 5}", qk_flat[:, u - 5, 3, :], qk_flat[:, u - 5, 2, :], 1.0)
                    if m and u >= 5:
                        for e in ((0, 1), (3, 4), (7, 8, 9))[u - 5]:
                            expert(it, e)
                if a:
                    scale_values(it, UNITS - 1)
                    vector_attn.end()
                if m:
                    for e in range(10, EXPERTS):
                        expert(it, e)
                if a:
                    apply_gate(it, 1)
                if m:
                    final_norm(it)
                    vector_moe.end()

            run_iterations(dve, iteration)

        @block.tensor
        def _(pe):
            pe.wait_ge(consts_made, 1)
            pe.wait_ge(edge_diff, 1)
            diff = edge_a.rearrange("e k c -> e (k c)")
            for k in range(BLOCKS):
                rows = min(P, WINDOW - P * k)
                last = pe.transpose(attended[0:rows, EDGES * k:EDGES * (k + 1)], diff[:, P * k:P * k + rows],
                                    ident[0:EDGES, 0:EDGES])
            last.then_inc(edge_turned, 1)
            pe.wait_ge(edge_turned_in, 2)
            pe.wait_ge(weights_in, WEIGHT_LOADS * DMA)
            for k in range(BLOCKS):
                rows = min(P, WINDOW - P * k)
                last = pe.matmul(experts_sum[C:C + EDGES, 0:C], edge_t[0:rows, k, :], wc[0:rows, k, :],
                                 start=(k == 0), stop=(k == BLOCKS - 1))
            last.then_inc(edge_conv, 1)
            pe.wait_ge(weights_made, 1)
            pe.wait_ge(bias_rows_in, 2 * DMA)

            def take(it, name):
                n = it.base + it.local[name]
                if it.register is not None or n >= 2:
                    value = n // 2
                    if it.register is not None:
                        value = it.register * (len(it.local) // 2) + value
                    if name == "turn4":
                        wait_apart(pe, bank_drained[n % 2], value)
                    else:
                        pe.wait_ge(bank_drained[n % 2], value)
                return bank(it, name)

            def parts(dst, hi, lo, rhs, n=1):
                pe.matmul(dst, hi, rhs, start=True, stop=False)
                return pe.matmul(dst, lo, rhs, start=False, stop=True)

            def query_key(b, u, pair):
                g, t = divmod(u, NT)
                if pair == 0 and t == 0:
                    pe.wait_ge(stack_in[g], b.count(5 * DMA, 5 * DMA))
                if u > 0 or not b.first():
                    pe.wait_ge(probs_ready, b.count(2 * UNITS, 2 * (u - 1) + pair + 1))
                for j in range(2 * pair, 2 * pair + 2):
                    h = GROUP * g + j
                    last = pe.matmul(scores[:, j, :], q_stack[:, h, P * t:P * (t + 1)], k_stack[:, h, :], start=True, stop=True)
                last.then_inc(scores_ready, 1)

            def sum_queries(b, u):
                g, t = divmod(u, NT)
                pe.wait_ge(v_scaled, b.count(UNITS, u + 1))
                if t == 0 and (g > 0 or not b.first()):
                    pe.wait_ge(gated_ready, b.count(GROUPS, g))
                for j in range(GROUP):
                    last = pe.matmul(attended[D * j:D * (j + 1), :], v_scaled_sb[:, u % 2, j, :], probs[:, u % 2, j, :],
                                     start=(t == 0), stop=(t == NT - 1), skip_group_check=True)
                last.then_inc(unit_summed, 1)

            def turn_rows(it, name, tile, rows=P):
                dst = take(it, name)
                for t in range(NT):
                    last = pe.transpose(dst[0:rows, P * t:P * (t + 1)], tile(t), ident[:])
                last.then_inc(bank_full, 1)

            def values(it, n):
                dst = take(it, f"v{n}")
                v = slice(2 * INNER, 3 * INNER)
                for j in range(2):
                    rows = n_split[:, P * (2 * n + j):P * (2 * n + j + 1)]
                    half = dst[:, INNER * j:INNER * (j + 1)]
                    pe.matmul(half, rows, w_qkv_hi[:, v], start=True, stop=False)
                    last = pe.matmul(half, rows, w_qkv_lo[:, v], start=False, stop=True)
                last.then_inc(bank_full, 1)

            def convolution(it):
                dst = take(it, "conv")
                for n, k in enumerate((0, 1, 2, 3, 4)):
                    rows = P if k < 4 else C + EDGES + 1
                    half = dst[C * (k % 2):C * (k % 2 + 1), :]
                    last = pe.matmul(half, wc[0:rows, k, :], turned[0:rows, k, :], start=(k < 2), stop=(k >= 3),
                                     skip_group_check=True)
                last.then_inc(bank_full, 1)

            def add_halves(it, name, tile):
                dst = take(it, name)
                for t in range(NT):
                    last = pe.matmul(dst[:, C * t:C * (t + 1)], tile[:, P * t:P * (t + 1)], halves[:], start=True, stop=True)
                last.then_inc(bank_full, 1)

            def project(it):
                dst = take(it, "project")
                for t in range(NT):
                    for g in range(GROUPS):
                        last = pe.matmul(dst[:, C * t:C * (t + 1)], gated[:, g, P * t:P * (t + 1)], half_wf[:, g, :],
                                         start=(g == 0), stop=(g == GROUPS - 1))
                last.then_inc(bank_full, 1)

            def router(it):
                dst = take(it, "router")
                for t in range(NT):
                    rows = f_split[:, P * t:P * (t + 1)]
                    cols = dst[:, EXPERTS * t:EXPERTS * (t + 1)]
                    pe.matmul(cols, rows, router_hi[:], start=True, stop=False)
                    last = pe.matmul(cols, rows, router_lo[:], start=False, stop=True)
                last.then_inc(bank_full, 1)

            def expert_out(it, e):
                drained(pe, it, f"e{e}")
                last = pe.matmul(experts_sum[C * (e % 2):C * (e % 2 + 1), :], w2_sb[:, e, :], hidden[:, e % 3, :],
                                 start=(e == 1), stop=(e >= EXPERTS - 2), skip_group_check=True)
                if e == EXPERTS - 1:
                    last.then_inc(experts_summed, 1)

            def expert(it, e):
                m = it.moe
                dst = take(it, f"e{e}")
                pe.matmul(dst, w1_hi[:, e, :], f_split[:], start=True, stop=False)
                pe.matmul(dst, w1_lo[:, e, :], f_ones[:], start=False, stop=True).then_inc(bank_full, 1)
                if e == 0:
                    if not m.first():
                        pe.wait_ge(moe_t_ready, m.count(1))
                    pe.matmul(experts_sum[0:C, :], b2_sb[:], share_t[:], start=True, stop=False, skip_group_check=True)
                else:
                    expert_out(it, e - 1)

            def iteration(it):
                a, k, m = it.attn, it.tok, it.moe
                for u in range(UNITS):
                    if a:
                        query_key(a, u, 0)
                    if u == 0:
                        if a:
                            values(it, 0)
                            values(it, 1)
                        if m:
                            pe.wait_ge(gated_ready, m.count(GROUPS, GROUPS))
                            project(it)
                    if u == 2:
                        if m:
                            pe.wait_ge(f_ready, m.count(1, 1))
                            turn_rows(it, "turn_f", lambda t: f_twice[:, t].rearrange("p a c -> p (a c)"))
                        if k:
                            pe.wait_ge(edges_marked, k.count(1, 1))
                            drained(pe, it, "turn3")
                            drained(pe, it, "turn4")
                            convolution(it)
                    if u == 4:
                        if m:
                            pe.wait_ge(share_ready, m.count(1, 1))
                            turn_rows(it, "turn_c", lambda t: share[:, t, :], EXPERTS)
                        if k:
                            pe.wait_ge(n_ready, k.count(1, 1))
                            turn_rows(it, "turn_n", lambda t: n_twice[:, t].rearrange("p a c -> p (a c)"))
                    if u in (5, 6) and k:
                        g = u - 5
                        if g == 0:
                            drained(pe, it, "turn_n")
                        w = slice(P * g, P * (g + 1))
                        parts(take(it, f"q{g}"), w_qkv_hi[:, w], w_qkv_lo[:, w], n_split[:]).then_inc(bank_full, 1)
                    if u == 6 and m:
                        expert(it, 2)
                    if u == 7 and m:
                        for e in (5, 6):
                            expert(it, e)
                    if a:
                        query_key(a, u, 1)
                        if u > 0:
                            sum_queries(a, u - 1)
                    if u == 0 and k:
                        pe.wait_ge(rows_gathered, k.count(NT * DMA, NT * DMA))
                        for n in range(3):
                            turn_rows(it, f"turn{n}", lambda t: gathered_rows[:, t, P * n:P * (n + 1)])
                    if u == 1 and k:
                        turn_rows(it, "turn3", lambda t: gathered_rows[:, t, 3 * P:4 * P])
                        turn_rows(it, "turn4", lambda t: gathered_rows[:, t, 4 * P:WINDOW], C)
                    if u == 2 and k:
                        drained(pe, it, "conv")
                        add_halves(it, "rows", conv_t)
                    if u == 3:
                        if m:
                            drained(pe, it, "turn_f")
                            router(it)
                        if a:
                            for g in range(GROUPS):
                                w = slice(P * g, P * (g + 1))
                                parts(take(it, f"gate{g}"), w_gate_hi[:, w], w_gate_lo[:, w], a_split[:]).then_inc(bank_full, 1)
                    if u == 4 and k:
                        turn_rows(it, "turn_a", lambda t: a_twice[:, t].rearrange("p a c -> p (a c)"))
                    if u in (5, 6) and k:
                        w = slice(INNER + P * (u - 5), INNER + P * (u - 4))
                        parts(take(it, f"k{u - 5}"), w_qkv_hi[:, w], w_qkv_lo[:, w], n_split[:]).then_inc(bank_full, 1)
                    if m and u >= 5:
                        for e in ((0, 1), (3, 4), (7, 8, 9))[u - 5]:
                            if e == 0:
                                drained(pe, it, "turn_c")
                            expert(it, e)
                if m:
                    for e in range(10, EXPERTS):
                        expert(it, e)
                    expert_out(it, EXPERTS - 1)
                if a:
                    sum_queries(a, UNITS - 1)
                if m:
                    pe.wait_ge(moe_t_ready, m.count(1, 1))
                    add_halves(it, "sum", moe_t)

            run_iterations(pe, iteration)


def kernel(**inputs):
    import numpy as np
    import concourse.bacc as bacc
    from concourse import mybir as mb
    from concourse.bass_utils import run_bass_kernel_spmd as run

    a = {name: np.asarray(value) for name, value in inputs.items()}
    row = lambda name: a[name].reshape(1, -1)
    arrays = {
        "x": a["x"],
        "emb": a["L0_tok_emb"],
        "conv_w": a["L0_tok_W"].transpose(2, 1, 0).reshape(WINDOW, C),
        "conv_b": row("L0_tok_b"),
        "ln_gamma": row("L0_attn_ln_gamma"),
        "ln_beta": row("L0_attn_ln_beta"),
        "w_qkv": a["L0_attn_W_qkv"].T,
        "w_gate": a["L0_attn_W_gate"].T,
        "b_gate": a["L0_attn_b_gate"].reshape(GROUPS, P).T,
        "w_final": a["L0_attn_W_final"].T,
        "b_final": row("L0_attn_b_final"),
        "router_w": a["L0_ffn_gate_w"],
        "router_b": row("L0_ffn_gate_b"),
        "w1": a["L0_ffn_w1"].transpose(1, 0, 2).reshape(C, EXPERTS * F),
        "b1": row("L0_ffn_b1"),
        "w2": a["L0_ffn_w2"].transpose(1, 0, 2).reshape(F, EXPERTS * C),
        "b2": a["L0_ffn_b2"],
        "gamma": row("L0_ffn_gamma"),
        "beta": row("L0_ffn_beta"),
    }
    arrays = {f"in_{name}": np.ascontiguousarray(v) for name, v in arrays.items()}
    nc = bacc.Bacc("TRN2", target_bir_lowering=False, num_devices=1)
    args = [nc.dram_tensor(name, v.shape, mb.dt.from_np(v.dtype), kind="ExternalInput").ap() for name, v in arrays.items()]
    out = nc.dram_tensor("out", (BATCHES, T, C), mb.dt.float32, kind="ExternalOutput").ap()
    tower_kernel(nc, *args, out)
    return run(nc, [arrays], core_ids=[0]).results[0]["out"]
```

```python
from contextlib import ExitStack

import concourse.bass as bass
from concourse import mybir

F32 = mybir.dt.float32
F32R = mybir.dt.float32r
I32 = mybir.dt.int32
ACT = mybir.ActivationFunctionType
ALU = mybir.AluOpType
X_AXIS = mybir.AxisListType.X

P = 128
BATCHES = 8
T = 512
NT = T // P
VOCAB = 50257
C = 64
TAPS = 9
WINDOW = TAPS * C
REACH = TAPS // 2
HEADS = 8
D = 32
GROUP = 4
GROUPS = HEADS // GROUP
INNER = HEADS * D
UNITS = GROUPS * NT
EXPERTS = 16
F = 128
EPS = 1e-5
SCALE = float(D) ** -0.5
BLOCKS = 5
EDGES = 2 * REACH
LOWER = -3e38
DMA = 16

FIRST_EXPERTS = 4
STEPS = 2

TENSOR_SLOTS = (
    "v0 v1 turn0 turn1",
    "last_unit turn2 turn3",
    "turn4 project",
    "conv1",
    "conv0 turn_f",
    "rows",
    "e4 e5 router",
    "gate1 gate0 e6",
    "e7 e8 turn_a",
    "turn_c turn_n",
    "e9 e10 q0 k0",
    "e11 q1 k1",
    "e12 e13 e14",
    "e15 out15",
    "sum e0",
    "e1 e2 e3",
)
SCALAR_SLOTS = (
    "v0 v1 turn0 turn1",
    "turn2 turn3",
    "turn4",
    "",
    "conv0 turn_f",
    "rows",
    "",
    "gate1 gate0 e_gap",
    "turn_a",
    "turn_n turn_c",
    "q0 k0",
    "q1 k1",
    "",
    "moe_t",
    "",
    "",
)
VECTOR_SLOTS = (
    "last_unit",
    "",
    "gated1",
    "marks h1",
    "norm_f",
    "turn_f",
    "e4 statistics_k e5",
    "norm_a best_two e6",
    "e7 e8 share_out",
    "turn_a",
    "turn_n e9 gated0 e10",
    "q0 k0 e11",
    "q1 k1 e12 e13 e14",
    "e15",
    "statistics_y e0 e1 norm_y",
    "e2 e3",
)
PART_OF = {name: part for part, names in {
    "tok": "turn0 turn1 turn2 turn3 turn4 conv1 conv0 rows turn_a turn_n q0 k0 q1 k1 marks statistics_k norm_a",
    "attn": "v0 v1 gate0 gate1 gated0",
    "moe": "last_unit gated1 project h1 norm_f turn_f router best_two e_gap share_out turn_c e0 e1 e2 e3",
    "late": "e4 e5 e6 e7 e8 e9 e10 e11 e12 e13 e14 e15 out15 moe_t sum statistics_y norm_y",
}.items() for name in names.split()}
NO_BANK = ("last_unit", "conv1", "out15")


def steps(slots, s, parts):
    return [name for name in slots[s].split() if PART_OF[name] in parts]


GATES = [name for slot in TENSOR_SLOTS for name in slot.split() if name.startswith("gate")]
USES = [(PART_OF[name], name) for slot in TENSOR_SLOTS for name in slot.split() if name not in NO_BANK]
ALL = ("tok", "attn", "moe", "late")


def uses_of(parts):
    return [name for part, name in USES if part in parts]


class Batch:

    def __init__(self, number, register=None):
        self.number, self.register, self.parity = number, register, number % 2

    def count(self, per, n=0):
        value = self.number * per + n
        return value if self.register is None else self.register * (STEPS * per) + value

    def index(self):
        return self.number if self.register is None else self.register * STEPS + self.number

    def first(self):
        return self.register is None and self.number == 0


class Iteration:

    def __init__(self, i, register=None):
        self.register = register
        self.parts = parts_of(i)
        self.base = sum(len(uses_of(parts_of(n))) for n in range(-1, i))
        batch = lambda part, number: Batch(number, register) if part in self.parts else None
        self.tok, self.attn, self.moe, self.late = (batch(part, i + 1 - n) for n, part in enumerate(ALL))
        names = uses_of(self.parts)
        self.position = {name: self.base + n for n, name in enumerate(names)}
        before = uses_of(parts_of(i - 1)) if i >= 0 else []
        self.position_before = {name: self.base - len(before) + n for n, name in enumerate(before)}
        self.next_use = self.base

    def above(self, per_iteration, value):
        return value if self.register is None else self.register * (STEPS * per_iteration) + value

    def full(self, name):
        return self.above(len(USES), self.position[name] + 1)

    def slot(self, name):
        return self.position[name] % 2

    def drained(self, position):
        return self.above(len(USES) // 2, position // 2 + 1)


def parts_of(i):
    return tuple(part for n, part in enumerate(ALL) if 0 <= i + 1 - n < BATCHES)


FIRST_LOOPED = len(ALL) - 1
LOOPS = (BATCHES - 1 - FIRST_LOOPED) // STEPS
assert len(USES) % 2 == 0


def run_iterations(engine, body):
    for i in range(-1, FIRST_LOOPED):
        body(Iteration(i))
    with engine.Fori(0, LOOPS) as j:
        for n in range(STEPS):
            body(Iteration(FIRST_LOOPED + n, j))
    for i in range(FIRST_LOOPED + LOOPS * STEPS, BATCHES + len(ALL) - 2):
        body(Iteration(i))


class Order:

    def __init__(self, sem, per):
        self.sem, self.per, self.n, self.batch = sem, per, 0, None

    def start(self, batch):
        self.n, self.batch = 0, batch

    def mark(self, instruction):
        instruction.then_inc(self.sem, 1)
        self.n += 1

    def value(self):
        assert self.n <= self.per
        return self.batch.count(self.per, self.n)

    def wait(self, engine):
        engine.wait_ge(self.sem, self.value())

    def end(self):
        assert self.n == self.per, (self.n, self.per)


def tower_kernel(nc, x, emb, edges, conv, by_channel, final, vectors, b1, w2, b2, out):
    with ExitStack() as ctx:
        def sb(name, shape, dtype=F32):
            return ctx.enter_context(nc.sbuf_tensor(name, shape, dtype))

        def sem(name):
            return ctx.enter_context(nc.semaphore(name))

        ident = sb("ident", [P, P])
        halves = sb("halves", [P, C])
        wc = sb("wc", [P, BLOCKS, C])
        w_qkv_hi, w_qkv_lo = sb("w_qkv_hi", [P, 3 * INNER], F32R), sb("w_qkv_lo", [P, 3 * INNER], F32R)
        w_gate_hi, w_gate_lo = sb("w_gate_hi", [P, INNER], F32R), sb("w_gate_lo", [P, INNER], F32R)
        router_hi, router_lo = sb("router_hi", [P, EXPERTS], F32R), sb("router_lo", [P, EXPERTS], F32R)
        halved = sb("halved", [P, GROUPS * C + GROUPS])
        half_wf = halved[:, 0:GROUPS * C].rearrange("p (g o) -> p g o", g=GROUPS)
        half_bg = halved[:, GROUPS * C:]
        w1_hi = sb("w1_hi", [P, EXPERTS, F], F32R)
        BIAS_ROWS = 2
        w1_lo = sb("w1_lo", [C + BIAS_ROWS, EXPERTS, F], F32R)
        w2_sb = sb("w2_sb", [P, EXPERTS, C])
        b2_sb = sb("b2_sb", [EXPERTS, C])
        vector_rows = sb("vector_rows", [P, 5 * C + EXPERTS])
        ln_g, ln_b, bf, ffn_g, ffn_b = (vector_rows[:, C * n:C * (n + 1)] for n in range(5))
        router_bias = vector_rows[:, 5 * C:]
        minus_half = sb("minus_half", [P, 2 * NT])
        expert_ids = sb("expert_ids", [P, EXPERTS])
        edge_ids = sb("edge_ids", [P, 2])
        windows = sb("windows", [P, (BATCHES + 1) * NT], I32)
        edge_t = sb("edge_t", [P, BLOCKS, EDGES])

        window_now = sb("window_now", [P, NT], I32)
        gathered_rows = sb("gathered_rows", [P, NT, WINDOW])
        turned = sb("turned", [P, BLOCKS, T])
        conv_t = sb("conv_t", [P, T])
        h0 = sb("h0", [P, NT, C])
        stats_k, mean_k = sb("stats_k", [P, NT, 6]), sb("mean_k", [P, NT, 2])
        var_k, rstd_k, inv_k = sb("var_k", [P, 2, NT]), sb("rstd_k", [P, 2, NT]), sb("inv_k", [P, NT])
        a_twice, n_twice = sb("a_twice", [P, NT, 2, C]), sb("n_twice", [P, NT, 2, C])
        n_hat = sb("n_hat", [P, NT, C])
        sum_next, sum_now = sb("sum_next", [P, NT, C]), sb("sum_now", [P, NT, C])
        n_split, a_split = sb("n_split", [P, T], F32R), sb("a_split", [P, T], F32R)
        qk_flat = sb("qk_flat", [P, GROUPS, 4, T], F32R)
        q_stack, k_stack = sb("q_stack", [P, HEADS, T], F32R), sb("k_stack", [P, HEADS, T], F32R)

        v_rows = sb("v_rows", [P, NT, INNER])
        gate = sb("gate", [P, GROUPS, T])
        neg_max, z, inv_z = sb("neg_max", [P, 2, GROUP]), sb("z", [P, 2, GROUP]), sb("inv_z", [P, 2, GROUP])
        probs = sb("probs", [P, 2, GROUP, T])
        v_scaled_sb = sb("v_scaled_sb", [P, 2, GROUP, D])

        h1 = sb("h1", [P, 2, NT, C])
        stats_m, mean_m = sb("stats_m", [P, NT, 6]), sb("mean_m", [P, NT, 2])
        var_m, rstd_m = sb("var_m", [P, NT]), sb("rstd_m", [P, NT])
        f_twice = sb("f_twice", [P, 2, NT, 2, C])
        f_split = sb("f_split", [P, 2, T], F32R)
        f_ones = sb("f_ones", [C + BIAS_ROWS, 2, T], F32R)
        logits, logits2 = sb("logits", [P, NT, EXPERTS]), sb("logits2", [P, NT, EXPERTS])
        same, cand = sb("same", [P, NT, EXPERTS]), sb("cand", [P, NT, EXPERTS])
        first_hot, second_hot = sb("first_hot", [P, NT, EXPERTS]), sb("second_hot", [P, NT, EXPERTS])
        top1, top2, which = sb("top1", [P, NT]), sb("top2", [P, NT]), sb("which", [P, NT])
        gap, e_gap, den, wt1, wt2 = (sb(n, [P, NT]) for n in ("gap", "e_gap", "den", "wt1", "wt2"))
        share = sb("share", [P, NT, EXPERTS])
        rows_tile = sb("rows_tile", [P, T])
        share_t, x_edge = rows_tile[0:EXPERTS], rows_tile[:].bitcast(I32)
        QUARTER = EXPERTS // 4
        share_row = sb("share_row", [P, QUARTER, T])
        share_all = sb("share_all", [P, EXPERTS, T])
        hidden = sb("hidden", [P, 3, T])
        moe_t = sb("moe_t", [P, T])
        stats_y, mean_y = sb("stats_y", [P, NT, 6]), sb("mean_y", [P, NT, 2])
        var_y, rstd_y = sb("var_y", [P, NT]), sb("rstd_y", [P, NT])
        y = sb("y", [P, NT, C])

        scratch = nc.dram_tensor("scratch", (GROUPS, 2, 2, D, GROUP, T), F32).ap()

        scores = ctx.enter_context(nc.psum_tensor("scores", [P, GROUP, T], F32))
        attended = ctx.enter_context(nc.psum_tensor("attended", [P, T], F32))
        experts_sum = ctx.enter_context(nc.psum_tensor("experts_sum", [P, T], F32))
        shared = ctx.enter_context(nc.psum_tensor("shared", [P, 2, T], F32))

        edges_in, x_in, conv_in, early_in = sem("edges_in"), sem("x_in"), sem("conv_in"), sem("early_in")
        weights_in = sem("weights_in")
        bias_rows_in = sem("bias_rows_in")
        consts_made, early_split, weights_made, bias_parts = (
            sem(n) for n in ("consts_made", "early_split", "weights_made", "bias_parts"))
        windows_made, edge_diff, edge_turned, edge_turned_in, edge_conv, edge_weights_in = (
            sem(n) for n in ("windows_made", "edge_diff", "edge_turned", "edge_turned_in", "edge_conv", "edge_weights_in"))
        bank_full = sem("bank_full")
        bank_drained = [sem("bank_drained0"), sem("bank_drained1")]
        window_copied = sem("window_copied")
        rows_gathered = sem("rows_gathered")
        x_edge_in = sem("x_edge_in")
        edges_marked = sem("edges_marked")
        var_k_ready, rstd_k_ready = sem("var_k_ready"), sem("rstd_k_ready")
        a_ready, n_ready = sem("a_ready"), sem("n_ready")
        high_k = sem("high_k")
        scratch_in = [sem("scratch_in0"), sem("scratch_in1")]
        stack_in = [sem("stack_in0"), sem("stack_in1")]
        scores_ready, max_ready, probs_ready = sem("scores_ready"), sem("max_ready"), sem("probs_ready")
        v_scaled, unit_summed = sem("v_scaled"), sem("unit_summed")
        gated_ready = sem("gated_ready")
        sum_made, sum_copied = sem("sum_made"), sem("sum_copied")
        var_f_ready, rstd_f_ready = sem("var_f_ready"), sem("rstd_f_ready")
        f_ready, high_f = sem("f_ready"), sem("high_f")
        gap_ready, e_gap_ready, share_ready = sem("gap_ready"), sem("e_gap_ready"), sem("share_ready")
        share_row_in, share_spread = sem("share_row_in"), sem("share_spread")
        experts_summed, moe_t_ready = sem("experts_summed"), sem("moe_t_ready")
        var_y_ready, rstd_y_ready, y_ready = sem("var_y_ready"), sem("rstd_y_ready"), sem("y_ready")
        result_ready, stored = sem("result_ready"), sem("stored")
        vector_setup, pool_setup = Order(sem("vector_setup"), 99), Order(sem("pool_setup"), 99)
        inverse_made = sem("inverse_made")
        vector_tok = Order(sem("vector_tok"), 14)
        vector_moe = Order(sem("vector_moe"), 27)
        vector_late = Order(sem("vector_late"), 11)
        pool_tok = Order(sem("pool_tok"), 3)
        pool_late = Order(sem("pool_late"), 2)

        stage = share_all[:].rearrange("p e t -> p (e t)")
        offset = [0]

        def staged(rows, n):
            view = stage[0:rows, offset[0]:offset[0] + n]
            offset[0] += n
            return view

        raw_qkv, raw_gate, raw_router, raw_w1 = staged(P, 3 * INNER), staged(P, INNER), staged(P, EXPERTS), staged(P, EXPERTS * F)
        EARLY = 4 * INNER
        raw_b1 = staged(1, EXPERTS * F)
        b1_hi, b1_lo = staged(1, EXPERTS * F).bitcast(F32R), raw_b1.bitcast(F32R)

        edge_windows = probs[0:EDGES].rearrange("e a h t -> e (a h t)")[:, 0:2 * WINDOW]
        edge_a, edge_b = edge_windows[:, 0:WINDOW], edge_windows[:, WINDOW:]

        block = ctx.enter_context(nc.Block())

        def bank(it, name):
            return shared[:, it.slot(name), :]

        def drained(engine, it, name):
            engine.wait_ge(bank_drained[it.slot(name)], it.drained(it.position[name]))

        def emptied(it, name):
            return [bank_drained[it.slot(name)], it.drained(it.position[name])]

        def in_register(engine, value):
            return value if isinstance(value, int) else engine.snap(engine.to_reg(value))

        def wait_apart(engine, *waits):
            values = [in_register(engine, value) for value in waits[1::2]]
            engine.wait_ge(consts_made, 1)
            for semaphore, value in zip(waits[::2], values):
                engine.wait_ge(semaphore, value)

        @block.sync
        def _(sp):
            sp.dma_start(windows[:, 0:BATCHES * NT].rearrange("p (b t) -> p b t", b=BATCHES),
                         x.rearrange("b (p t) -> p b t", t=NT)).then_inc(x_in, DMA)
            sp.dma_start(windows[:, BATCHES * NT:], x[BATCHES - 1].rearrange("(p t) -> p t", t=NT)).then_inc(x_in, DMA)
            sp.dma_start(edge_windows, edges).then_inc(edges_in, DMA)

            def move_bias_parts():
                sp.wait_ge(bias_parts, 2)
                for n, part in enumerate((b1_hi, b1_lo)):
                    sp.dma_start(w1_lo[C + n:C + n + 1].rearrange("p e f -> p (e f)").bitcast(F32),
                                 part.bitcast(F32)).then_inc(bias_rows_in, DMA)

            def load_x_edge(k):
                if not k.first():
                    sp.wait_ge(edges_marked, k.count(1))
                row = x[k.number:k.number + 1, :] if k.register is None else x[bass.ds(k.index(), 1), :]
                sp.dma_start(x_edge[C:C + EDGES, :], row.to_broadcast([EDGES, T])).then_inc(x_edge_in, DMA)

            def stack(it, g):
                k = it.tok
                for name in (f"q{g}", f"k{g}"):
                    wait_apart(sp, *emptied(it, name))
                if not k.first():
                    sp.wait_ge(stack_in[g], k.count(5 * DMA))
                for side in range(2):
                    for part in range(2):
                        sp.dma_start(scratch[g, side, part].rearrange("d h n -> h d n"),
                                     qk_flat[:, g, 2 * side + part, :].bitcast(F32)).then_inc(scratch_in[g], DMA)
                if not k.first():
                    scored = in_register(sp, Batch(k.number - 1, k.register).count(2 * UNITS, 2 * NT * (g + 1)))
                sp.wait_ge(scratch_in[g], k.count(4 * DMA, 4 * DMA))
                if not k.first():
                    sp.wait_ge(scores_ready, scored)
                heads = slice(GROUP * g, GROUP * (g + 1))
                for lo in (0, 2 * D):
                    sp.dma_start(q_stack[lo:lo + 2 * D, heads, :].bitcast(F32),
                                 scratch[g, 0].rearrange("s d h n -> (s d) h n")).then_inc(stack_in[g], DMA)
                sp.dma_start(k_stack[0:2 * D, heads, :].bitcast(F32),
                             scratch[g, 1].rearrange("s d h n -> (s d) h n")).then_inc(stack_in[g], DMA)
                sp.dma_start(k_stack[2 * D:3 * D, heads, :].bitcast(F32), scratch[g, 1, 1]).then_inc(stack_in[g], DMA)
                sp.dma_start(k_stack[3 * D:4 * D, heads, :].bitcast(F32), scratch[g, 1, 0]).then_inc(stack_in[g], DMA)

            def iteration(it):
                if it.tok:
                    load_x_edge(it.tok)
                if it.attn and it.attn.first():
                    move_bias_parts()
                if it.moe:
                    m = it.moe
                    wait_apart(sp, *emptied(it, "turn_c"))
                    if not m.first():
                        sp.wait_ge(share_spread, m.count(4))
                    for g in range(4):
                        sp.dma_start(share_row[32 * g:32 * g + 1, :, :],
                                     share_t[QUARTER * g:QUARTER * (g + 1), :]).then_inc(share_row_in, DMA)
                if it.tok:
                    for g in range(GROUPS):
                        stack(it, g)
                if it.late:
                    m = it.late
                    sp.wait_ge(result_ready, m.count(1, 1))
                    rows = out[m.number] if m.register is None else out[bass.ds(m.index(), 1)].rearrange("a n c -> (a n) c")
                    sp.dma_start(rows.rearrange("(p t) c -> p (t c)", t=NT),
                                 y[:].rearrange("p t c -> p (t c)")).then_inc(stored, DMA)

            run_iterations(sp, iteration)
            sp.wait_ge(stored, DMA * BATCHES)

        @block.gpsimd
        def _(pool):
            pool_setup.start(Batch(0))
            pool_setup.mark(pool.memset(ident[:], 0.0))
            pool_setup.mark(pool.iota(edge_ids[:, 0:1].bitcast(I32), pattern=[[0, 1]], base=-C, channel_multiplier=1))
            pool_setup.mark(pool.iota(expert_ids[:].bitcast(I32), pattern=[[1, EXPERTS]], base=-EXPERTS, channel_multiplier=0))
            pool_setup.mark(pool.memset(minus_half[:], -0.5))
            pool_setup.wait(pool)
            pool.affine_select(out=ident[:], in_=ident[:], compare_op=ALU.not_equal, fill=1.0, base=0,
                               pattern=[[-1, P]], channel_multiplier=1).then_inc(consts_made, 1)

            def gather(k, rows_turned=None):
                if not k.first():
                    wait_apart(pool, rows_gathered, k.count(NT * DMA), bank_full, rows_turned)
                else:
                    pool.wait_ge(windows_made, 1)
                start = k.index() * NT
                cols = windows[:, start:start + NT] if k.register is None else windows[:, bass.ds(start, NT)]
                pool.tensor_copy(window_now[:], cols).then_inc(window_copied, 1)
                wait_apart(pool, window_copied, k.count(1, 1))
                for t in range(NT):
                    pool.indirect_dma_start(
                        out=gathered_rows[:, t, :], out_offset=None, in_=emb,
                        in_offset=bass.IndirectOffsetOnAxis(ap=window_now[:, t:t + 1], axis=0),
                    ).then_inc(rows_gathered, DMA)

            gather(Batch(0))

            def spread(it, g):
                m = it.moe
                waits = []
                if g == 0:
                    if k_gathers(it):
                        waits += [rows_gathered, it.tok.count(NT * DMA, 2 * NT * DMA)]
                    if it.late:
                        waits += emptied(it, "e4") + emptied(it, "e5")
                    waits += [share_row_in, m.count(4 * DMA, 4 * DMA)]
                else:
                    if it.late:
                        waits += emptied(it, f"e{QUARTER * (g + 1) - 2}") + emptied(it, f"e{QUARTER * (g + 1) - 1}")
                    if it.late and g == 1:
                        waits += [result_ready, it.late.count(1, 1)]
                    waits += [share_spread, m.count(4, g)]
                wait_apart(pool, *waits)
                pool.partition_broadcast(share_all[:, QUARTER * g:QUARTER * (g + 1), :].rearrange("p e t -> p (e t)"),
                                         share_row[32 * g:32 * g + 1, :, :].rearrange("p e t -> p (e t)")
                                         ).then_inc(share_spread, 1)

            def k_gathers(it):
                return it.tok and (it.register is not None or it.tok.number + 1 < BATCHES)

            def iteration(it):
                a, k, m, late = it.attn, it.tok, it.moe, it.late
                if k_gathers(it):
                    gather(Batch(k.number + 1, k.register), it.full("turn4"))
                if a:
                    wait_apart(pool, sum_made, a.count(1, 1), *(emptied(it, "project") if m else []))
                    pool.tensor_copy(sum_now[:], sum_next[:]).then_inc(sum_copied, 1)
                if m:
                    wait_apart(pool, var_f_ready, m.count(1, 1))
                    pool.tensor_tensor(rstd_m[:], var_m[:], minus_half[:, 0:NT], ALU.pow).then_inc(rstd_f_ready, 1)
                if k:
                    pool_tok.start(k)
                    wait_apart(pool, var_k_ready, k.count(1, 1))
                    pool.tensor_tensor(rstd_k[:].rearrange("p a t -> p (a t)"), var_k[:].rearrange("p a t -> p (a t)"),
                                       minus_half[:], ALU.pow).then_inc(rstd_k_ready, 1)
                    pool.wait_ge(a_ready, k.count(1, 1))
                    pool.wait_ge(rstd_k_ready, k.count(1, 1))
                    if k.first():
                        pool.wait_ge(weights_in, 6 * DMA)
                    pool_tok.mark(pool.tensor_tensor(n_hat[:], a_twice[:, :, 0, :],
                                                     rstd_k[:, 1, :, None].to_broadcast([P, NT, C]), ALU.mult))
                    pool_tok.wait(pool)
                    pool_tok.mark(pool.tensor_tensor(n_hat[:], n_hat[:], ln_g[:, None, :].to_broadcast([P, NT, C]), ALU.mult))
                    pool_tok.wait(pool)
                    pool.tensor_tensor(n_twice[:], n_hat[:, :, None, :].to_broadcast([P, NT, 2, C]),
                                       ln_b[:, None, None, :].to_broadcast([P, NT, 2, C]), ALU.add).then_inc(n_ready, 1)
                    if not k.first():
                        pool.wait_ge(sum_copied, k.count(1))
                    pool_tok.mark(pool.tensor_tensor(sum_next[:], h0[:], a_twice[:, :, 0, :], ALU.add))
                    pool_tok.wait(pool)
                    pool_tok.end()
                    pool.tensor_tensor(sum_next[:], sum_next[:], bf[:, None, :].to_broadcast([P, NT, C]), ALU.add
                                       ).then_inc(sum_made, 1)
                if m:
                    spread(it, 0)
                if late:
                    pool_late.start(late)
                    wait_apart(pool, var_y_ready, late.count(1, 1), *((share_spread, m.count(4, 1)) if m else ()))
                    pool.tensor_tensor(rstd_y[:], var_y[:], minus_half[:, 0:NT], ALU.pow).then_inc(rstd_y_ready, 1)
                    pool.wait_ge(y_ready, late.count(1, 1))
                    pool_late.mark(pool.tensor_tensor(y[:], y[:], ffn_g[:, None, :].to_broadcast([P, NT, C]), ALU.mult))
                    pool_late.wait(pool)
                    pool_late.mark(pool.tensor_tensor(y[:], y[:], ffn_b[:, None, :].to_broadcast([P, NT, C]), ALU.add))
                    pool_late.wait(pool)
                    pool_late.end()
                    pool.tensor_tensor(y[:], y[:], h1[:, late.parity], ALU.add).then_inc(result_ready, 1)
                if m:
                    for g in range(1, 4):
                        spread(it, g)
                    wait_apart(pool, share_spread, m.count(4, 4))

            run_iterations(pool, iteration)

        @block.scalar
        def _(act):
            act.dma_start(wc[:].rearrange("p b o -> p (b o)"), conv).then_inc(conv_in, DMA)
            act.dma_start(stage[:, 0:EARLY], by_channel[:, 0:EARLY]).then_inc(early_in, DMA)
            for dst, src in ((vector_rows[:], vectors.to_broadcast([P, vectors.shape[1]])), (halved[:], final), (raw_b1, b1),
                             (stage[:, EARLY:by_channel.shape[1]], by_channel[:, EARLY:]),
                             (w2_sb[:].rearrange("p e o -> p (e o)"), w2), (b2_sb[:], b2)):
                act.dma_start(dst, src).then_inc(weights_in, DMA)

            def copy_out(it, name, dst, src):
                act.wait_ge(bank_full, it.full(name))
                nc.scalar.activation(dst, src, ACT.Copy).then_inc(bank_drained[it.slot(name)], 1)

            def exponentials(b, u, pair):
                act.wait_ge(max_ready, b.count(2 * UNITS, 2 * u + pair + 1))
                if u >= 2 or not b.first():
                    act.wait_ge(unit_summed, b.count(UNITS, u - 1))
                for j in range(2 * pair, 2 * pair + 2):
                    last = nc.scalar.activation(probs[:, u % 2, j, :], scores[:, j, :], ACT.Exp,
                                                bias=neg_max[:, u % 2, j:j + 1], accum_out=z[:, u % 2, j:j + 1])
                last.then_inc(probs_ready, 1)

            def high_part(it, name, dst, scale=1.0):
                act.wait_ge(bank_full, it.full(name))
                return nc.scalar.activation(dst, bank(it, name), ACT.Copy, scale=scale)

            def step(it, name):
                a, k, m = it.attn, it.tok, it.moe
                if name in ("v0", "v1"):
                    n = int(name[1:])
                    if n == 0 and not a.first():
                        act.wait_ge(v_scaled, a.count(UNITS))
                    copy_out(it, name, v_rows[:, 2 * n:2 * n + 2, :].rearrange("p t c -> p (t c)"), bank(it, name))
                elif name in ("turn0", "turn1", "turn2", "turn3"):
                    copy_out(it, name, turned[:, int(name[4:]), :], bank(it, name))
                elif name == "turn4":
                    copy_out(it, name, turned[0:C, 4, :], bank(it, name)[0:C, :])
                elif name == "conv0":
                    copy_out(it, name, conv_t[:], bank(it, name))
                elif name == "rows":
                    if not k.first():
                        act.wait_ge(sum_made, k.count(1))
                    copy_out(it, name, h0[:].rearrange("p t c -> p (t c)"), bank(it, name)[:, 0:NT * C])
                elif name == "turn_f":
                    high_part(it, name, f_split[:, m.parity])
                    nc.scalar.activation(f_ones[0:C, m.parity], bank(it, name)[0:C, :], ACT.Copy).then_inc(high_f, 1)
                elif name in ("gate0", "gate1"):
                    g = int(name[4:])
                    if a.first():
                        act.wait_ge(weights_made, 1)
                    elif name == GATES[0]:
                        act.wait_ge(gated_ready, a.count(GROUPS))
                    act.wait_ge(bank_full, it.full(name))
                    nc.scalar.activation(gate[:, g, :], bank(it, name), ACT.Tanh, bias=half_bg[:, g:g + 1],
                                         scale=0.5).then_inc(bank_drained[it.slot(name)], 1)
                elif name == "e_gap":
                    act.wait_ge(gap_ready, m.count(1, 1))
                    nc.scalar.activation(e_gap[:], gap[:], ACT.Exp).then_inc(e_gap_ready, 1)
                elif name in ("turn_a", "turn_n"):
                    high_part(it, name, (a_split if name == "turn_a" else n_split)[:]).then_inc(high_k, 1)
                elif name == "turn_c":
                    if not m.first():
                        act.wait_ge(share_row_in, m.count(4 * DMA))
                    copy_out(it, name, share_t, bank(it, name)[0:EXPERTS, :])
                elif name in ("q0", "q1"):
                    g = int(name[1:])
                    if not k.first():
                        act.wait_ge(scratch_in[g], k.count(4 * DMA))
                    high_part(it, name, qk_flat[:, g, 0, :], SCALE).then_inc(high_k, 1)
                elif name in ("k0", "k1"):
                    high_part(it, name, qk_flat[:, int(name[1:]), 2, :]).then_inc(high_k, 1)
                else:
                    assert name == "moe_t"
                    act.wait_ge(experts_summed, it.late.count(1, 1))
                    nc.scalar.activation(moe_t[:], experts_sum[:], ACT.Copy).then_inc(moe_t_ready, 1)

            def iteration(it):
                for s in range(2 * UNITS):
                    if it.attn:
                        exponentials(it.attn, s // 2, s % 2)
                    for name in steps(SCALAR_SLOTS, s, it.parts):
                        step(it, name)

            run_iterations(act, iteration)

        @block.vector
        def _(dve):
            vector_setup.start(Batch(0))
            mark = vector_setup.mark

            def wait():
                vector_setup.wait(dve)

            mark(dve.memset(turned[C:P, BLOCKS - 1, :], 1.0))
            mark(dve.memset(f_ones[C:C + BIAS_ROWS].rearrange("p a t -> p (a t)").bitcast(F32), 1.0))
            dve.wait_ge(x_in, 2 * DMA)
            mark(dve.tensor_scalar(windows[:], windows[:], REACH, 0, ALU.subtract, ALU.max))
            wait()
            dve.tensor_scalar(windows[:], windows[:], VOCAB - TAPS, None, ALU.min).then_inc(windows_made, 1)
            dve.wait_ge(consts_made, 1)
            ids = edge_ids[:, 0:1]
            mark(dve.tensor_copy(edge_ids[:, 1:2], ids.bitcast(I32)))
            mark(dve.tensor_copy(same[:, 0, :], expert_ids[:].bitcast(I32)))
            wait()
            mark(dve.tensor_copy(expert_ids[:], same[:, 0, :]))
            mark(dve.tensor_scalar(ids, edge_ids[:, 1:2], REACH - 0.5, VOCAB - EDGES, ALU.is_ge, ALU.mult))
            wait()
            mark(dve.tensor_tensor(ids, ids, edge_ids[:, 1:2], ALU.add))
            mark(dve.tensor_tensor(halves[:], ident[:, 0:C], ident[:, C:P], ALU.add))
            dve.wait_ge(edges_in, DMA)
            dve.tensor_tensor(edge_a, edge_a, edge_b, ALU.subtract).then_inc(edge_diff, 1)

            def split(pairs):
                for hi, lo, raw in pairs:
                    mark(dve.tensor_copy(hi, raw))
                wait()
                for hi, lo, raw in pairs:
                    rows = lo.shape[0]
                    last = dve.tensor_tensor(lo, raw[0:rows], hi[0:rows], ALU.subtract)
                    mark(last) if lo is not pairs[-1][1] else None
                return last

            dve.wait_ge(early_in, DMA)
            split(((w_qkv_hi[:], w_qkv_lo[:], raw_qkv), (w_gate_hi[:], w_gate_lo[:], raw_gate))).then_inc(early_split, 1)
            dve.wait_ge(edge_turned, 1)
            full = BLOCKS - 1
            dve.tensor_copy(edge_t[:, 0:full, :], attended[:, 0:full * EDGES].rearrange("p (k e) -> p k e", e=EDGES)
                            ).then_inc(edge_turned_in, 1)
            dve.tensor_copy(edge_t[0:C, full, :], attended[0:C, full * EDGES:BLOCKS * EDGES]).then_inc(edge_turned_in, 1)
            dve.wait_ge(edge_conv, 1)
            dve.tensor_copy(wc[C:C + EDGES, 4, :], experts_sum[C:C + EDGES, 0:C]).then_inc(edge_weights_in, 1)

            def late_weights():
                dve.wait_ge(weights_in, 6 * DMA)
                dve.tensor_copy(b1_hi, raw_b1).then_inc(bias_parts, 1)
                dve.wait_ge(bias_parts, 1)
                dve.tensor_tensor(b1_lo, raw_b1, b1_hi, ALU.subtract).then_inc(bias_parts, 1)
                mark(dve.tensor_scalar(halved[:], halved[:], 0.5, None, ALU.mult))
                split(((router_hi[:], router_lo[:], raw_router),
                       (w1_hi[:].rearrange("p e f -> p (e f)"), w1_lo[0:C].rearrange("p e f -> p (e f)"), raw_w1))
                      ).then_inc(weights_made, 1)

            def maxima(b, u, pair):
                dve.wait_ge(scores_ready, b.count(2 * UNITS, 2 * u + pair + 1))
                dve.tensor_reduce(neg_max[:, u % 2, 2 * pair:2 * pair + 2], scores[:, 2 * pair:2 * pair + 2, :], X_AXIS,
                                  ALU.max, negate=True).then_inc(max_ready, 1)

            def scale_values(it, b, u):
                dve.wait_ge(probs_ready, b.count(2 * UNITS, 2 * u + 2))
                if u >= 2 or not b.first():
                    dve.wait_ge(unit_summed, b.count(UNITS, u - 1))
                dve.reciprocal(inv_z[:, u % 2, :], z[:, u % 2, :]).then_inc(inverse_made, 1)
                if u == 0:
                    drained(dve, it, "v0")
                    drained(dve, it, "v1")
                dve.wait_ge(inverse_made, b.count(UNITS, u + 1))
                g, t = divmod(u, NT)
                dve.tensor_tensor(v_scaled_sb[:, u % 2], v_rows[:, t, g * P:(g + 1) * P].rearrange("p (h d) -> p h d", d=D),
                                  inv_z[:, u % 2, :, None].to_broadcast([P, GROUP, D]), ALU.mult).then_inc(v_scaled, 1)

            def apply_gate(it, b, g):
                dve.wait_ge(unit_summed, b.count(UNITS, NT * (g + 1)))
                if g == 0:
                    drained(dve, it, "gate0")
                    drained(dve, it, "gate1")
                dve.scalar_tensor_tensor(gate[:, g, :], gate[:, g, :], 1.0, attended[:], ALU.add, ALU.mult
                                         ).then_inc(gated_ready, 1)

            def statistics(order, src, stats, mean):
                for t in range(NT):
                    order.mark(dve.bn_stats(stats[:, t, :], src[:, t, :]))
                wait_apart(dve, order.sem, order.value())
                for t in range(NT):
                    order.mark(dve.bn_aggr(mean[:, t, :], stats[:, t, :]))
                order.wait(dve)

            def normalise(dst, src, mean, rstd):
                for t in range(NT):
                    last = dve.tensor_scalar(dst(t), src(t), mean[:, t, 0:1], rstd(t), ALU.subtract, ALU.mult)
                    yield last

            def twice(tile, t):
                return tile[:, t, None, :].to_broadcast([P, 2, C])

            def low_part(it, name, dst, high, scale=None):
                src = bank(it, name)[C:P, :] if scale is None else bank(it, name)
                if scale is None or scale == 1.0:
                    ins = dve.tensor_tensor(dst, src, high, ALU.subtract)
                else:
                    ins = dve.scalar_tensor_tensor(dst, src, scale, high, ALU.mult, ALU.subtract)
                ins.then_inc(bank_drained[it.slot(name)], 1)

            def mark_edges(k):
                dve.wait_ge(x_edge_in, k.count(DMA, DMA))
                if not k.first():
                    dve.wait_ge(rstd_k_ready, k.count(1))
                dve.tensor_scalar(turned[C:C + EDGES, 4, :].rearrange("e (t p) -> e p t", t=NT),
                                  x_edge[C:C + EDGES, :].rearrange("e (p t) -> e p t", t=NT),
                                  edge_ids[C:C + EDGES, 0:1], None, ALU.is_equal).then_inc(edges_marked, 1)

            def statistics_k(it):
                k = it.tok
                o = vector_tok
                o.start(k)
                drained(dve, it, "rows")
                statistics(o, h0, stats_k, mean_k)
                var = mean_k[:, :, 1]
                o.mark(dve.tensor_scalar(var_k[:, 0, :], var, EPS, None, ALU.add))
                o.wait(dve)
                o.mark(dve.reciprocal(inv_k[:], var_k[:, 0, :]))
                o.wait(dve)
                o.mark(dve.tensor_tensor(inv_k[:], inv_k[:], var, ALU.mult))
                o.wait(dve)
                dve.tensor_scalar(var_k[:, 1, :], inv_k[:], EPS, None, ALU.add).then_inc(var_k_ready, 1)

            def norm_a(it):
                k, o = it.tok, vector_tok
                dve.wait_ge(rstd_k_ready, k.count(1, 1))
                if not k.first():
                    dve.wait_ge(sum_made, k.count(1))
                ins = list(normalise(lambda t: a_twice[:, t], lambda t: twice(h0, t), mean_k, lambda t: rstd_k[:, 0, t:t + 1]))
                for one in ins[:-1]:
                    o.mark(one)
                ins[-1].then_inc(a_ready, 1)
                o.end()

            def norm_f_statistics(it):
                m = it.moe
                o = vector_moe
                o.start(m)
                dve.wait_ge(bank_full, it.full("project"))
                dve.wait_ge(sum_copied, m.count(1, 1))
                if m.register is not None or m.number >= 2:
                    dve.wait_ge(result_ready, m.count(1, -1))
                dve.tensor_tensor(h1[:, m.parity].rearrange("p t c -> p (t c)"), bank(it, "project")[:, 0:NT * C],
                                  sum_now[:].rearrange("p t c -> p (t c)"), ALU.add).then_inc(bank_drained[it.slot("project")], 1)
                drained(dve, it, "project")
                statistics(o, h1[:, m.parity], stats_m, mean_m)
                dve.tensor_scalar(var_m[:], mean_m[:, :, 1], EPS, None, ALU.add).then_inc(var_f_ready, 1)

            def norm_f(it):
                m = it.moe
                dve.wait_ge(rstd_f_ready, m.count(1, 1))
                ins = list(normalise(lambda t: f_twice[:, m.parity, t], lambda t: twice(h1[:, m.parity], t), mean_m, lambda t: rstd_m[:, t:t + 1]))
                for one in ins[:-1]:
                    vector_moe.mark(one)
                ins[-1].then_inc(f_ready, 1)
                dve.wait_ge(f_ready, m.count(1, 1))

            wide = [P, NT, EXPERTS]

            def best_two(it):
                m = it.moe
                o = vector_moe
                dve.wait_ge(bank_full, it.full("router"))
                dve.tensor_tensor(logits[:], bank(it, "router")[:, 0:NT * EXPERTS].rearrange("p (t e) -> p t e", e=EXPERTS),
                                  router_bias[:, None, :].to_broadcast(wide), ALU.add).then_inc(bank_drained[it.slot("router")], 1)
                drained(dve, it, "router")

                def best(src, top, hot):
                    o.mark(dve.tensor_reduce(top[:], src[:], X_AXIS, ALU.max))
                    o.wait(dve)
                    o.mark(dve.tensor_tensor(same[:], src[:], top[:, :, None].to_broadcast(wide), ALU.is_equal))
                    o.wait(dve)
                    o.mark(dve.tensor_tensor(cand[:], same[:], expert_ids[:, None, :].to_broadcast(wide), ALU.mult))
                    o.wait(dve)
                    o.mark(dve.tensor_reduce(which[:], cand[:], X_AXIS, ALU.min))
                    o.wait(dve)
                    o.mark(dve.tensor_tensor(hot[:], expert_ids[:, None, :].to_broadcast(wide),
                                             which[:, :, None].to_broadcast(wide), ALU.is_equal))
                    o.wait(dve)

                best(logits, top1, first_hot)
                o.mark(dve.scalar_tensor_tensor(logits2[:], first_hot[:], LOWER, logits[:], ALU.mult, ALU.add))
                o.wait(dve)
                best(logits2, top2, second_hot)
                dve.tensor_tensor(gap[:], top2[:], top1[:], ALU.subtract).then_inc(gap_ready, 1)

            def share_out(it):
                m, o = it.moe, vector_moe
                dve.wait_ge(e_gap_ready, m.count(1, 1))
                o.mark(dve.tensor_scalar(den[:], e_gap[:], 1.0, None, ALU.add))
                o.wait(dve)
                o.mark(dve.reciprocal(wt1[:], den[:]))
                o.wait(dve)
                o.mark(dve.tensor_tensor(wt2[:], e_gap[:], wt1[:], ALU.mult))
                o.mark(dve.tensor_tensor(same[:], first_hot[:], wt1[:, :, None].to_broadcast(wide), ALU.mult))
                o.wait(dve)
                o.mark(dve.tensor_tensor(cand[:], second_hot[:], wt2[:, :, None].to_broadcast(wide), ALU.mult))
                o.wait(dve)
                dve.tensor_tensor(share[:], same[:], cand[:], ALU.add).then_inc(share_ready, 1)

            def expert(it, e):
                m = it.moe if e < FIRST_EXPERTS else it.late
                dve.wait_ge(bank_full, it.full(f"e{e}"))
                if e % QUARTER == 0:
                    dve.wait_ge(share_spread, m.count(4, e // QUARTER + 1))
                dve.scalar_tensor_tensor(hidden[:, e % 3, :], bank(it, f"e{e}"), 0.0, share_all[:, e, :], ALU.max, ALU.mult
                                         ).then_inc(bank_drained[it.slot(f"e{e}")], 1)

            def final_statistics(it):
                late, o = it.late, vector_late
                o.start(late)
                if not late.first():
                    dve.wait_ge(stored, late.count(DMA))
                dve.wait_ge(bank_full, it.full("sum"))
                dve.tensor_tensor(y[:], bank(it, "sum")[:, 0:NT * C].rearrange("p (t c) -> p t c", c=C),
                                  f_twice[:, late.parity, :, 0, :], ALU.add).then_inc(bank_drained[it.slot("sum")], 1)
                drained(dve, it, "sum")
                statistics(o, y, stats_y, mean_y)
                dve.tensor_scalar(var_y[:], mean_y[:, :, 1], EPS, None, ALU.add).then_inc(var_y_ready, 1)

            def final_norm(it):
                late, o = it.late, vector_late
                dve.wait_ge(rstd_y_ready, late.count(1, 1))
                ins = list(normalise(lambda t: y[:, t, :], lambda t: y[:, t, :], mean_y, lambda t: rstd_y[:, t:t + 1]))
                for one in ins[:-1]:
                    o.mark(one)
                ins[-1].then_inc(y_ready, 1)
                o.end()

            def step(it, name):
                a, k, m, late = it.attn, it.tok, it.moe, it.late
                if name[0] == "e":
                    expert(it, int(name[1:]))
                elif name == "last_unit":
                    scale_values(it, m, UNITS - 1)
                elif name in ("gated0", "gated1"):
                    g = int(name[5:])
                    apply_gate(it, a if g == 0 else m, g)
                elif name == "h1":
                    norm_f_statistics(it)
                elif name == "marks":
                    mark_edges(k)
                elif name == "norm_f":
                    norm_f(it)
                elif name == "turn_f":
                    dve.wait_ge(high_f, m.count(1, 1))
                    low_part(it, name, f_split[C:P, m.parity], f_split[C:P, m.parity])
                elif name == "statistics_k":
                    statistics_k(it)
                elif name == "norm_a":
                    norm_a(it)
                elif name == "best_two":
                    best_two(it)
                elif name == "share_out":
                    share_out(it)
                elif name in ("turn_a", "turn_n"):
                    first = name == "turn_a"
                    dve.wait_ge(high_k, k.count(6, 1 if first else 2))
                    half = (a_split if first else n_split)[C:P, :]
                    low_part(it, name, half, half)
                elif name in ("q0", "q1", "k0", "k1"):
                    g, side = int(name[1:]), "qk".index(name[0])
                    dve.wait_ge(high_k, k.count(6, 3 + 2 * g + side))
                    low_part(it, name, qk_flat[:, g, 2 * side + 1, :], qk_flat[:, g, 2 * side, :], (SCALE, 1.0)[side])
                elif name == "statistics_y":
                    final_statistics(it)
                else:
                    assert name == "norm_y"
                    final_norm(it)

            def iteration(it):
                a = it.attn
                if a and a.first():
                    late_weights()
                for s in range(2 * UNITS):
                    u, pair = divmod(s, 2)
                    if a:
                        maxima(a, u, pair)
                        if pair == 0 and u > 0:
                            scale_values(it, a, u - 1)
                    for name in steps(VECTOR_SLOTS, s, it.parts):
                        step(it, name)

            run_iterations(dve, iteration)

        @block.tensor
        def _(pe):
            def edge_weights():
                pe.wait_ge(consts_made, 1)
                pe.wait_ge(edge_diff, 1)
                for k in range(BLOCKS):
                    rows = min(P, WINDOW - P * k)
                    last = pe.transpose(attended[0:rows, EDGES * k:EDGES * (k + 1)], edge_a[:, P * k:P * k + rows],
                                        ident[0:EDGES, 0:EDGES])
                last.then_inc(edge_turned, 1)
                pe.wait_ge(edge_turned_in, 2)
                pe.wait_ge(conv_in, DMA)
                for k in range(BLOCKS):
                    rows = min(P, WINDOW - P * k)
                    last = pe.matmul(experts_sum[C:C + EDGES, 0:C], edge_t[0:rows, k, :], wc[0:rows, k, :],
                                     start=(k == 0), stop=(k == BLOCKS - 1))
                last.then_inc(edge_conv, 1)

            pe.wait_ge(consts_made, 1)

            def take(it, name):
                position = it.position[name]
                assert position == it.next_use, name
                it.next_use += 1
                if it.register is not None or position >= 2:
                    value = it.drained(position - 2)
                    if name == "turn4":
                        wait_apart(pe, bank_drained[position % 2], value)
                    else:
                        pe.wait_ge(bank_drained[position % 2], value)
                return bank(it, name)

            def parts(dst, hi, lo, rhs, n=1):
                pe.matmul(dst, hi, rhs, start=True, stop=False)
                return pe.matmul(dst, lo, rhs, start=False, stop=True)

            def query_key(b, u, pair):
                g, t = divmod(u, NT)
                if pair == 0 and t == 0:
                    pe.wait_ge(stack_in[g], b.count(5 * DMA, 5 * DMA))
                if u > 0 or not b.first():
                    pe.wait_ge(probs_ready, b.count(2 * UNITS, 2 * (u - 1) + pair + 1))
                for j in range(2 * pair, 2 * pair + 2):
                    h = GROUP * g + j
                    last = pe.matmul(scores[:, j, :], q_stack[:, h, P * t:P * (t + 1)], k_stack[:, h, :], start=True, stop=True)
                last.then_inc(scores_ready, 1)

            def sum_queries(b, u):
                g, t = divmod(u, NT)
                pe.wait_ge(v_scaled, b.count(UNITS, u + 1))
                if t == 0 and (g > 0 or not b.first()):
                    pe.wait_ge(gated_ready, b.count(GROUPS, g))
                for j in range(GROUP):
                    last = pe.matmul(attended[D * j:D * (j + 1), :], v_scaled_sb[:, u % 2, j, :], probs[:, u % 2, j, :],
                                     start=(t == 0), stop=(t == NT - 1), skip_group_check=True)
                last.then_inc(unit_summed, 1)

            def turn_rows(it, name, tile, rows=P):
                dst = take(it, name)
                for t in range(NT):
                    last = pe.transpose(dst[0:rows, P * t:P * (t + 1)], tile(t), ident[:])
                last.then_inc(bank_full, 1)

            def values(it, n):
                dst = take(it, f"v{n}")
                v = slice(2 * INNER, 3 * INNER)
                for j in range(2):
                    rows = n_split[:, P * (2 * n + j):P * (2 * n + j + 1)]
                    half = dst[:, INNER * j:INNER * (j + 1)]
                    pe.matmul(half, rows, w_qkv_hi[:, v], start=True, stop=False)
                    last = pe.matmul(half, rows, w_qkv_lo[:, v], start=False, stop=True)
                last.then_inc(bank_full, 1)

            def convolution(it, half):
                dst = take(it, "conv0") if half == 1 else bank(it, "conv0")
                for k in range(half, BLOCKS, 2):
                    rows = P if k < BLOCKS - 1 else C + EDGES + 1
                    last = pe.matmul(dst[C * half:C * (half + 1), :], wc[0:rows, k, :], turned[0:rows, k, :],
                                     start=(k == half), stop=(k + 2 >= BLOCKS), skip_group_check=True)
                if half == 0:
                    last.then_inc(bank_full, 1)

            def add_halves(it, name, tile):
                dst = take(it, name)
                for t in range(NT):
                    last = pe.matmul(dst[:, C * t:C * (t + 1)], tile[:, P * t:P * (t + 1)], halves[:], start=True, stop=True)
                last.then_inc(bank_full, 1)

            def project(it):
                dst = take(it, "project")
                for t in range(NT):
                    for g in range(GROUPS):
                        last = pe.matmul(dst[:, C * t:C * (t + 1)], gate[:, g, P * t:P * (t + 1)], half_wf[:, g, :],
                                         start=(g == 0), stop=(g == GROUPS - 1))
                last.then_inc(bank_full, 1)

            def router(it):
                dst = take(it, "router")
                for t in range(NT):
                    rows = f_split[:, it.moe.parity, P * t:P * (t + 1)]
                    cols = dst[:, EXPERTS * t:EXPERTS * (t + 1)]
                    pe.matmul(cols, rows, router_hi[:], start=True, stop=False)
                    last = pe.matmul(cols, rows, router_lo[:], start=False, stop=True)
                last.then_inc(bank_full, 1)

            def expert_out(it, e, positions):
                position = positions[f"e{e}"]
                pe.wait_ge(bank_drained[position % 2], it.drained(position))
                last = pe.matmul(experts_sum[C * (e % 2):C * (e % 2 + 1), :], w2_sb[:, e, :], hidden[:, e % 3, :],
                                 start=(e == 1), stop=(e >= EXPERTS - 2), skip_group_check=True)
                if e == EXPERTS - 1:
                    last.then_inc(experts_summed, 1)

            def expert(it, e):
                m = it.moe if e < FIRST_EXPERTS else it.late
                if e == FIRST_EXPERTS:
                    expert_out(it, e - 1, it.position_before)
                dst = take(it, f"e{e}")
                pe.matmul(dst, w1_hi[:, e, :], f_split[:, m.parity], start=True, stop=False)
                pe.matmul(dst, w1_lo[:, e, :], f_ones[:, m.parity], start=False, stop=True).then_inc(bank_full, 1)
                if e == 0:
                    if not m.first():
                        pe.wait_ge(moe_t_ready, m.count(1))
                    pe.matmul(experts_sum[0:C, :], b2_sb[:], share_t, start=True, stop=False, skip_group_check=True)
                elif e != FIRST_EXPERTS:
                    expert_out(it, e - 1, it.position)

            def step(it, name):
                a, k, m, late = it.attn, it.tok, it.moe, it.late
                if name[0] == "e":
                    if name == "e0":
                        drained(pe, it, "turn_c")
                    expert(it, int(name[1:]))
                elif name in ("v0", "v1"):
                    values(it, int(name[1:]))
                elif name in ("turn0", "turn1", "turn2", "turn3"):
                    n = int(name[4:])
                    if n == 0:
                        pe.wait_ge(rows_gathered, k.count(NT * DMA, NT * DMA))
                    turn_rows(it, name, lambda t: gathered_rows[:, t, P * n:P * (n + 1)])
                elif name == "turn4":
                    turn_rows(it, name, lambda t: gathered_rows[:, t, 4 * P:WINDOW], C)
                elif name == "last_unit":
                    sum_queries(m, UNITS - 1)
                elif name == "project":
                    pe.wait_ge(gated_ready, m.count(GROUPS, GROUPS))
                    project(it)
                elif name == "conv1":
                    if k.first():
                        edge_weights()
                    drained(pe, it, "turn3")
                    convolution(it, 1)
                elif name == "conv0":
                    pe.wait_ge(edges_marked, k.count(1, 1))
                    if k.first():
                        pe.wait_ge(edge_weights_in, 1)
                    drained(pe, it, "turn4")
                    convolution(it, 0)
                elif name == "rows":
                    drained(pe, it, "conv0")
                    add_halves(it, name, conv_t)
                elif name == "turn_f":
                    pe.wait_ge(f_ready, m.count(1, 1))
                    turn_rows(it, name, lambda t: f_twice[:, m.parity, t].rearrange("p a c -> p (a c)"))
                elif name == "router":
                    drained(pe, it, "turn_f")
                    router(it)
                elif name in ("gate0", "gate1"):
                    w = slice(P * int(name[4:]), P * (int(name[4:]) + 1))
                    parts(take(it, name), w_gate_hi[:, w], w_gate_lo[:, w], a_split[:]).then_inc(bank_full, 1)
                elif name == "turn_a":
                    pe.wait_ge(a_ready, k.count(1, 1))
                    turn_rows(it, name, lambda t: a_twice[:, t].rearrange("p a c -> p (a c)"))
                elif name == "turn_c":
                    pe.wait_ge(share_ready, m.count(1, 1))
                    turn_rows(it, name, lambda t: share[:, t, :], EXPERTS)
                elif name == "turn_n":
                    pe.wait_ge(n_ready, k.count(1, 1))
                    turn_rows(it, name, lambda t: n_twice[:, t].rearrange("p a c -> p (a c)"))
                elif name in ("q0", "q1", "k0", "k1"):
                    first = INNER * "qk".index(name[0]) + P * int(name[1:])
                    w = slice(first, first + P)
                    if name == "q0":
                        if k.first():
                            pe.wait_ge(early_split, 1)
                        drained(pe, it, "turn_n")
                    parts(take(it, name), w_qkv_hi[:, w], w_qkv_lo[:, w], n_split[:]).then_inc(bank_full, 1)
                elif name == "out15":
                    expert_out(it, EXPERTS - 1, it.position)
                else:
                    assert name == "sum"
                    pe.wait_ge(moe_t_ready, late.count(1, 1))
                    add_halves(it, name, moe_t)

            def iteration(it):
                a = it.attn
                if it.moe and it.moe.first():
                    pe.wait_ge(weights_made, 1)
                    pe.wait_ge(bias_rows_in, 2 * DMA)
                for s in range(2 * UNITS):
                    if a:
                        for ahead in ((0, 1) if s == 0 else (s + 1,) if s + 1 < 2 * UNITS else ()):
                            query_key(a, ahead // 2, ahead % 2)
                        if s % 2 == 1 and s > 1:
                            sum_queries(a, s // 2 - 1)
                    for name in steps(TENSOR_SLOTS, s, it.parts):
                        step(it, name)

            run_iterations(pe, iteration)


def kernel(**inputs):
    import numpy as np
    import concourse.bacc as bacc
    from concourse import mybir as mb
    from concourse.bass_utils import run_bass_kernel_spmd as run

    a = {name: np.asarray(value) for name, value in inputs.items()}
    row = lambda *names: np.concatenate([a[name].reshape(1, -1) for name in names], 1)
    ends = np.r_[0:REACH, VOCAB - REACH:VOCAB][:, None]
    taps = np.arange(TAPS)
    cut_off = np.clip(ends - REACH + taps, 0, VOCAB - 1)
    gathered = np.clip(ends - REACH, 0, VOCAB - TAPS) + taps
    conv = np.zeros((BLOCKS * P, C), a["L0_tok_W"].dtype)
    conv[0:WINDOW] = a["L0_tok_W"].transpose(2, 1, 0).reshape(WINDOW, C)
    conv[WINDOW + EDGES] = a["L0_tok_b"]
    by_channel = np.concatenate([a["L0_attn_W_qkv"].T, a["L0_attn_W_gate"].T, a["L0_ffn_gate_w"],
                                 a["L0_ffn_w1"].transpose(1, 0, 2).reshape(C, EXPERTS * F)], 1)
    arrays = {
        "x": a["x"],
        "emb": a["L0_tok_emb"],
        "edges": np.concatenate([a["L0_tok_emb"][rows].reshape(EDGES, WINDOW) for rows in (cut_off, gathered)], 1),
        "conv": conv.reshape(BLOCKS, P, C).transpose(1, 0, 2).reshape(P, BLOCKS * C),
        "by_channel": np.concatenate([by_channel, by_channel], 0),
        "final": np.concatenate([a["L0_attn_W_final"].T.reshape(GROUPS, P, C).transpose(1, 0, 2).reshape(P, GROUPS * C),
                                 a["L0_attn_b_gate"].reshape(GROUPS, P).T], 1),
        "vectors": row("L0_attn_ln_gamma", "L0_attn_ln_beta", "L0_attn_b_final", "L0_ffn_gamma", "L0_ffn_beta", "L0_ffn_gate_b"),
        "b1": row("L0_ffn_b1"),
        "w2": a["L0_ffn_w2"].transpose(1, 0, 2).reshape(F, EXPERTS * C),
        "b2": a["L0_ffn_b2"],
    }
    arrays = {f"in_{name}": np.ascontiguousarray(v) for name, v in arrays.items()}
    nc = bacc.Bacc("TRN2", target_bir_lowering=False, num_devices=1)
    args = [nc.dram_tensor(name, v.shape, mb.dt.from_np(v.dtype), kind="ExternalInput").ap() for name, v in arrays.items()]
    out = nc.dram_tensor("out", (BATCHES, T, C), mb.dt.float32, kind="ExternalOutput").ap()
    tower_kernel(nc, *args, out)
    return run(nc, [arrays], core_ids=[0]).results[0]["out"]
```

```python
from contextlib import ExitStack

import concourse.bass as bass
from concourse import mybir

F32 = mybir.dt.float32
F32R = mybir.dt.float32r
I32 = mybir.dt.int32
ACT = mybir.ActivationFunctionType
ALU = mybir.AluOpType
X_AXIS = mybir.AxisListType.X

P = 128
BATCHES = 8
T = 512
NT = T // P
VOCAB = 50257
C = 64
TAPS = 9
WINDOW = TAPS * C
REACH = TAPS // 2
HEADS = 8
D = 32
GROUP = 4
GROUPS = HEADS // GROUP
INNER = HEADS * D
SCORES = GROUPS * NT * GROUP
UNITS = GROUPS * NT
EXPERTS = 16
F = 128
EPS = 1e-5
SCALE = float(D) ** -0.5
BLOCKS = 5
EDGES = 2 * REACH
LOWER = -3e38
DMA = 16

LAG = 2
FIRST_EXPERTS = 4
EARLY_SPREADS = 2
BANKS = 3
STEPS = 2

TENSOR_SLOTS = (
    "v0 v1 turn0 last_unit",
    "turn1 turn2 turn3",
    "turn4 project conv1",
    "",
    "conv0 turn_f",
    "rows",
    "e4 e5 router",
    "gate1 gate0 e6",
    "e7 e8 turn_a",
    "turn_c turn_n",
    "e9 e10 q0 k0",
    "e11 q1 k1",
    "e12 e13 e14",
    "e15 out15 e1",
    "sum e0",
    "e2 e3",
)
SCALAR_SLOTS = (
    "v0 v1 turn0",
    "turn1 turn2 turn3",
    "turn4",
    "conv1",
    "conv0 turn_f",
    "rows",
    "",
    "gate1 gate0 e_gap",
    "turn_a",
    "turn_n turn_c",
    "q0 k0",
    "q1 k1",
    "",
    "moe_t",
    "",
    "",
)
VECTOR_SLOTS = (
    "last_unit last_unit",
    "gated1",
    "scale scale",
    "marks h1 h1 h1 h1",
    "scale scale norm_f norm_f",
    "turn_f",
    "scale scale e4 statistics_k statistics_k statistics_k statistics_k statistics_k statistics_k e5",
    "best_two best_two best_two best_two best_two best_two best_two best_two best_two best_two best_two "
    "best_two best_two e6 norm_a share_out",
    "scale scale norm_a e7 e8 share_out share_out share_out share_out",
    "turn_a",
    "scale scale turn_n e9 gated0 e10",
    "q0 k0 e11",
    "scale scale q1 k1 e12 e13 e14",
    "e15",
    "scale scale e1 statistics_y statistics_y statistics_y statistics_y e0",
    "norm_y norm_y e3 e2",
)
PART_OF = {name: part for part, names in {
    "tok": "turn0 turn1 turn2 turn3 turn4 conv1 conv0 rows turn_a turn_n q0 k0 q1 k1 marks statistics_k norm_a",
    "attn": "v0 v1 gate0 gate1 gated0 scale",
    "moe": "last_unit gated1 project h1 norm_f turn_f router best_two e_gap share_out turn_c e0 e1 e2 e3",
    "late": "e4 e5 e6 e7 e8 e9 e10 e11 e12 e13 e14 e15 out15 moe_t sum statistics_y norm_y",
}.items() for name in names.split()}
NO_BANK = ("last_unit", "out15")


def steps(slots, s, parts):
    return [name for name in slots[s].split() if PART_OF[name] in parts]


GATES = [name for slot in TENSOR_SLOTS for name in slot.split() if name.startswith("gate")]
USES = [(PART_OF[name], name) for slot in TENSOR_SLOTS for name in slot.split() if name not in NO_BANK]
ALL = ("tok", "attn", "moe", "late")


def uses_of(parts):
    return [name for part, name in USES if part in parts]


class Batch:

    def __init__(self, number, register=None):
        self.number, self.register, self.parity = number, register, number % 2

    def count(self, per, n=0):
        value = self.number * per + n
        return value if self.register is None else self.register * (STEPS * per) + value

    def index(self):
        return self.number if self.register is None else self.register * STEPS + self.number

    def first(self):
        return self.register is None and self.number == 0


class Iteration:

    def __init__(self, i, register=None):
        self.register = register
        self.parts = parts_of(i)
        self.base = sum(len(uses_of(parts_of(n))) for n in range(-1, i))
        batch = lambda part, number: Batch(number, register) if part in self.parts else None
        self.tok, self.attn, self.moe, self.late = (batch(part, i + 1 - n) for n, part in enumerate(ALL))
        names = uses_of(self.parts)
        self.position = {name: self.base + n for n, name in enumerate(names)}
        before = uses_of(parts_of(i - 1)) if i >= 0 else []
        self.position_before = {name: self.base - len(before) + n for n, name in enumerate(before)}
        self.next_use = self.base
        self.begun = {}

    def above(self, per_iteration, value):
        return value if self.register is None else self.register * (STEPS * per_iteration) + value

    def full(self, name):
        return self.above(len(USES), self.position[name] + 1)

    def slot(self, name):
        return self.position[name] % BANKS

    def drained(self, position):
        return self.above(len(USES) // BANKS, position // BANKS + 1)


def parts_of(i):
    return tuple(part for n, part in enumerate(ALL) if 0 <= i + 1 - n < BATCHES)


FIRST_LOOPED = len(ALL) - 1
LOOPS = (BATCHES - 1 - FIRST_LOOPED) // STEPS
assert len(USES) % BANKS == 0


def run_iterations(engine, body):
    for i in range(-1, FIRST_LOOPED):
        body(Iteration(i))
    with engine.Fori(0, LOOPS) as j:
        for n in range(STEPS):
            body(Iteration(FIRST_LOOPED + n, j))
    for i in range(FIRST_LOOPED + LOOPS * STEPS, BATCHES + len(ALL) - 2):
        body(Iteration(i))


class Order:

    def __init__(self, sem, per):
        self.sem, self.per, self.n, self.batch = sem, per, 0, None

    def start(self, batch):
        self.n, self.batch = 0, batch

    def mark(self, instruction):
        instruction.then_inc(self.sem, 1)
        self.n += 1

    def value(self):
        assert self.n <= self.per
        return self.batch.count(self.per, self.n)

    def wait(self, engine):
        engine.wait_ge(self.sem, self.value())

    def end(self):
        assert self.n == self.per, (self.n, self.per)


def tower_kernel(nc, x, emb, edges, conv, by_channel, final, vectors, b1, w2, b2, out):
    with ExitStack() as ctx:
        def sb(name, shape, dtype=F32):
            return ctx.enter_context(nc.sbuf_tensor(name, shape, dtype))

        def sem(name):
            return ctx.enter_context(nc.semaphore(name))

        ident = sb("ident", [P, P])
        halves = sb("halves", [P, C])
        wc = sb("wc", [P, BLOCKS, C])
        w_qkv_hi, w_qkv_lo = sb("w_qkv_hi", [P, 3 * INNER], F32R), sb("w_qkv_lo", [P, 3 * INNER], F32R)
        w_gate_hi, w_gate_lo = sb("w_gate_hi", [P, INNER], F32R), sb("w_gate_lo", [P, INNER], F32R)
        router_hi, router_lo = sb("router_hi", [P, EXPERTS], F32R), sb("router_lo", [P, EXPERTS], F32R)
        halved = sb("halved", [P, GROUPS * C + GROUPS])
        half_wf = halved[:, 0:GROUPS * C].rearrange("p (g o) -> p g o", g=GROUPS)
        half_bg = halved[:, GROUPS * C:]
        w1_hi = sb("w1_hi", [P, EXPERTS, F], F32R)
        BIAS_ROWS = 2
        w1_lo = sb("w1_lo", [C + BIAS_ROWS, EXPERTS, F], F32R)
        w2_sb = sb("w2_sb", [P, EXPERTS, C])
        b2_sb = sb("b2_sb", [EXPERTS, C])
        vector_rows = sb("vector_rows", [P, 5 * C + EXPERTS])
        ln_g, ln_b, bf, ffn_g, ffn_b = (vector_rows[:, C * n:C * (n + 1)] for n in range(5))
        router_bias = vector_rows[:, 5 * C:]
        minus_half = sb("minus_half", [P, 2 * NT])
        expert_ids = sb("expert_ids", [P, EXPERTS])
        edge_ids = sb("edge_ids", [P, 2])
        windows = sb("windows", [P, (BATCHES + 1) * NT], I32)
        edge_t = sb("edge_t", [P, BLOCKS, EDGES])

        window_now = sb("window_now", [P, NT], I32)
        gathered_rows = sb("gathered_rows", [P, NT, WINDOW])
        turned = sb("turned", [P, BLOCKS, T])
        conv_t = sb("conv_t", [P, T])
        h0 = sb("h0", [P, NT, C])
        stats_k, mean_k = sb("stats_k", [P, NT, 6]), sb("mean_k", [P, NT, 2])
        var_k, rstd_k, inv_k = sb("var_k", [P, 2, NT]), sb("rstd_k", [P, 2, NT]), sb("inv_k", [P, NT])
        a_twice, n_twice = sb("a_twice", [P, NT, 2, C]), sb("n_twice", [P, NT, 2, C])
        n_hat = sb("n_hat", [P, NT, C])
        sum_next, sum_now = sb("sum_next", [P, NT, C]), sb("sum_now", [P, NT, C])
        n_split, a_split = sb("n_split", [P, T], F32R), sb("a_split", [P, T], F32R)
        qk_flat = sb("qk_flat", [P, GROUPS, 4, T], F32R)
        q_stack, k_stack = sb("q_stack", [P, HEADS, T], F32R), sb("k_stack", [P, HEADS, T], F32R)

        v_rows = sb("v_rows", [P, NT, INNER])
        gate = sb("gate", [P, GROUPS, T])
        neg_max, z, inv_z = sb("neg_max", [P, 2, GROUP]), sb("z", [P, 2, GROUP]), sb("inv_z", [P, 2, GROUP])
        probs = sb("probs", [P, 2, GROUP, T])
        v_scaled_sb = sb("v_scaled_sb", [P, 2, GROUP, D])

        h1 = sb("h1", [P, 2, NT, C])
        stats_m, mean_m = sb("stats_m", [P, NT, 6]), sb("mean_m", [P, NT, 2])
        var_m, rstd_m = sb("var_m", [P, NT]), sb("rstd_m", [P, NT])
        f_twice = sb("f_twice", [P, 2, NT, 2, C])
        f_split = sb("f_split", [P, 2, T], F32R)
        f_ones = sb("f_ones", [C + BIAS_ROWS, 2, T], F32R)
        logits, logits2 = sb("logits", [P, NT, EXPERTS]), sb("logits2", [P, NT, EXPERTS])
        same, cand = sb("same", [P, NT, EXPERTS]), sb("cand", [P, NT, EXPERTS])
        first_hot, second_hot = sb("first_hot", [P, NT, EXPERTS]), sb("second_hot", [P, NT, EXPERTS])
        top1, top2, which = sb("top1", [P, NT]), sb("top2", [P, NT]), sb("which", [P, NT])
        gap, e_gap, den, wt1, wt2 = (sb(n, [P, NT]) for n in ("gap", "e_gap", "den", "wt1", "wt2"))
        share = sb("share", [P, NT, EXPERTS])
        rows_tile = sb("rows_tile", [P, T])
        share_t, x_edge = rows_tile[0:EXPERTS], rows_tile[:].bitcast(I32)
        QUARTER = EXPERTS // 4
        share_row = sb("share_row", [P, QUARTER, T])
        share_all = sb("share_all", [P, EXPERTS, T])
        hidden = sb("hidden", [P, 3, T])
        moe_t = sb("moe_t", [P, T])
        stats_y, mean_y = sb("stats_y", [P, NT, 6]), sb("mean_y", [P, NT, 2])
        var_y, rstd_y = sb("var_y", [P, NT]), sb("rstd_y", [P, NT])
        y = sb("y", [P, NT, C])

        scratch = nc.dram_tensor("scratch", (GROUPS, 2, 2, D, GROUP, T), F32).ap()

        scores = ctx.enter_context(nc.psum_tensor("scores", [P, BANKS, T], F32))
        attended = ctx.enter_context(nc.psum_tensor("attended", [P, T], F32))
        experts_sum = ctx.enter_context(nc.psum_tensor("experts_sum", [P, T], F32))
        shared = ctx.enter_context(nc.psum_tensor("shared", [P, BANKS, T], F32))

        edges_in, x_in, conv_in, early_in = sem("edges_in"), sem("x_in"), sem("conv_in"), sem("early_in")
        weights_in = sem("weights_in")
        bias_rows_in = sem("bias_rows_in")
        consts_made, early_split, weights_made, bias_parts = (
            sem(n) for n in ("consts_made", "early_split", "weights_made", "bias_parts"))
        windows_made, edge_diff, edge_turned, edge_turned_in, edge_conv, edge_weights_in = (
            sem(n) for n in ("windows_made", "edge_diff", "edge_turned", "edge_turned_in", "edge_conv", "edge_weights_in"))
        bank_full = sem("bank_full")
        bank_drained = [sem(f"bank_drained{n}") for n in range(BANKS)]
        window_copied = sem("window_copied")
        rows_gathered = sem("rows_gathered")
        x_edge_in = sem("x_edge_in")
        edges_marked = sem("edges_marked")
        var_k_ready, rstd_k_ready = sem("var_k_ready"), sem("rstd_k_ready")
        a_ready, n_ready = sem("a_ready"), sem("n_ready")
        high_k = sem("high_k")
        scratch_in = [sem("scratch_in0"), sem("scratch_in1")]
        stack_in = [sem("stack_in0"), sem("stack_in1")]
        scores_ready, max_ready, probs_ready = sem("scores_ready"), sem("max_ready"), sem("probs_ready")
        v_scaled, unit_summed = sem("v_scaled"), sem("unit_summed")
        gated_ready = sem("gated_ready")
        sum_made, sum_copied = sem("sum_made"), sem("sum_copied")
        var_f_ready, rstd_f_ready = sem("var_f_ready"), sem("rstd_f_ready")
        f_ready, high_f = sem("f_ready"), sem("high_f")
        gap_ready, e_gap_ready, share_ready = sem("gap_ready"), sem("e_gap_ready"), sem("share_ready")
        share_row_in, share_spread = sem("share_row_in"), sem("share_spread")
        experts_summed, moe_t_ready = sem("experts_summed"), sem("moe_t_ready")
        var_y_ready, rstd_y_ready, y_ready = sem("var_y_ready"), sem("rstd_y_ready"), sem("y_ready")
        result_ready, stored = sem("result_ready"), sem("stored")
        vector_setup, pool_setup = Order(sem("vector_setup"), 99), Order(sem("pool_setup"), 99)
        inverse_made = sem("inverse_made")
        vector_tok = Order(sem("vector_tok"), 14)
        vector_moe = Order(sem("vector_moe"), 27)
        vector_late = Order(sem("vector_late"), 11)
        pool_tok = Order(sem("pool_tok"), 3)
        pool_late = Order(sem("pool_late"), 2)

        stage = share_all[:].rearrange("p e t -> p (e t)")
        offset = [0]

        def staged(rows, n):
            view = stage[0:rows, offset[0]:offset[0] + n]
            offset[0] += n
            return view

        raw_qkv, raw_gate, raw_router, raw_w1 = staged(P, 3 * INNER), staged(P, INNER), staged(P, EXPERTS), staged(P, EXPERTS * F)
        EARLY = 4 * INNER
        raw_b1 = staged(1, EXPERTS * F)
        b1_hi, b1_lo = staged(1, EXPERTS * F).bitcast(F32R), raw_b1.bitcast(F32R)

        edge_windows = probs[0:EDGES].rearrange("e a h t -> e (a h t)")[:, 0:2 * WINDOW]
        edge_a, edge_b = edge_windows[:, 0:WINDOW], edge_windows[:, WINDOW:]

        block = ctx.enter_context(nc.Block())

        def bank(it, name):
            return shared[:, it.slot(name), :]

        def drained(engine, it, name):
            engine.wait_ge(bank_drained[it.slot(name)], it.drained(it.position[name]))

        def emptied(it, name):
            return [bank_drained[it.slot(name)], it.drained(it.position[name])]

        def in_register(engine, value):
            return value if isinstance(value, int) else engine.snap(engine.to_reg(value))

        def wait_apart(engine, *waits):
            values = [in_register(engine, value) for value in waits[1::2]]
            engine.wait_ge(consts_made, 1)
            for semaphore, value in zip(waits[::2], values):
                engine.wait_ge(semaphore, value)

        @block.sync
        def _(sp):
            sp.dma_start(windows[:, 0:BATCHES * NT].rearrange("p (b t) -> p b t", b=BATCHES),
                         x.rearrange("b (p t) -> p b t", t=NT)).then_inc(x_in, DMA)
            sp.dma_start(windows[:, BATCHES * NT:], x[BATCHES - 1].rearrange("(p t) -> p t", t=NT)).then_inc(x_in, DMA)
            sp.dma_start(edge_windows, edges).then_inc(edges_in, DMA)

            def move_bias_parts():
                sp.wait_ge(bias_parts, 2)
                for n, part in enumerate((b1_hi, b1_lo)):
                    sp.dma_start(w1_lo[C + n:C + n + 1].rearrange("p e f -> p (e f)").bitcast(F32),
                                 part.bitcast(F32)).then_inc(bias_rows_in, DMA)

            def load_x_edge(k):
                if not k.first():
                    sp.wait_ge(edges_marked, k.count(1))
                row = x[k.number:k.number + 1, :] if k.register is None else x[bass.ds(k.index(), 1), :]
                sp.dma_start(x_edge[C:C + EDGES, :], row.to_broadcast([EDGES, T])).then_inc(x_edge_in, DMA)

            def stack(it, g):
                k = it.tok
                for name in (f"q{g}", f"k{g}"):
                    wait_apart(sp, *emptied(it, name))
                if not k.first():
                    sp.wait_ge(stack_in[g], k.count(5 * DMA))
                for side in range(2):
                    for part in range(2):
                        sp.dma_start(scratch[g, side, part].rearrange("d h n -> h d n"),
                                     qk_flat[:, g, 2 * side + part, :].bitcast(F32)).then_inc(scratch_in[g], DMA)
                if not k.first():
                    scored = in_register(sp, Batch(k.number - 1, k.register).count(SCORES, GROUP * NT * (g + 1)))
                sp.wait_ge(scratch_in[g], k.count(4 * DMA, 4 * DMA))
                if not k.first():
                    sp.wait_ge(scores_ready, scored)
                heads = slice(GROUP * g, GROUP * (g + 1))
                for lo in (0, 2 * D):
                    sp.dma_start(q_stack[lo:lo + 2 * D, heads, :].bitcast(F32),
                                 scratch[g, 0].rearrange("s d h n -> (s d) h n")).then_inc(stack_in[g], DMA)
                sp.dma_start(k_stack[0:2 * D, heads, :].bitcast(F32),
                             scratch[g, 1].rearrange("s d h n -> (s d) h n")).then_inc(stack_in[g], DMA)
                sp.dma_start(k_stack[2 * D:3 * D, heads, :].bitcast(F32), scratch[g, 1, 1]).then_inc(stack_in[g], DMA)
                sp.dma_start(k_stack[3 * D:4 * D, heads, :].bitcast(F32), scratch[g, 1, 0]).then_inc(stack_in[g], DMA)

            def iteration(it):
                if it.tok:
                    load_x_edge(it.tok)
                if it.attn and it.attn.first():
                    move_bias_parts()
                if it.moe:
                    m = it.moe
                    wait_apart(sp, *emptied(it, "turn_c"))
                    if not m.first():
                        sp.wait_ge(share_spread, m.count(4))
                    for g in range(4):
                        sp.dma_start(share_row[32 * g:32 * g + 1, :, :],
                                     share_t[QUARTER * g:QUARTER * (g + 1), :]).then_inc(share_row_in, DMA)
                if it.tok:
                    for g in range(GROUPS):
                        stack(it, g)
                if it.late:
                    m = it.late
                    sp.wait_ge(result_ready, m.count(1, 1))
                    rows = out[m.number] if m.register is None else out[bass.ds(m.index(), 1)].rearrange("a n c -> (a n) c")
                    sp.dma_start(rows.rearrange("(p t) c -> p (t c)", t=NT),
                                 y[:].rearrange("p t c -> p (t c)")).then_inc(stored, DMA)

            run_iterations(sp, iteration)
            sp.wait_ge(stored, DMA * BATCHES)

        @block.gpsimd
        def _(pool):
            pool_setup.start(Batch(0))
            pool_setup.mark(pool.memset(ident[:], 0.0))
            pool_setup.mark(pool.iota(edge_ids[:, 0:1].bitcast(I32), pattern=[[0, 1]], base=-C, channel_multiplier=1))
            pool_setup.mark(pool.iota(expert_ids[:].bitcast(I32), pattern=[[1, EXPERTS]], base=-EXPERTS, channel_multiplier=0))
            pool_setup.mark(pool.memset(minus_half[:], -0.5))
            pool_setup.wait(pool)
            pool.affine_select(out=ident[:], in_=ident[:], compare_op=ALU.not_equal, fill=1.0, base=0,
                               pattern=[[-1, P]], channel_multiplier=1).then_inc(consts_made, 1)

            def gather(k, rows_turned=None):
                if not k.first():
                    wait_apart(pool, rows_gathered, k.count(NT * DMA), bank_full, rows_turned)
                else:
                    pool.wait_ge(windows_made, 1)
                start = k.index() * NT
                cols = windows[:, start:start + NT] if k.register is None else windows[:, bass.ds(start, NT)]
                pool.tensor_copy(window_now[:], cols).then_inc(window_copied, 1)
                wait_apart(pool, window_copied, k.count(1, 1))
                for t in range(NT):
                    pool.indirect_dma_start(
                        out=gathered_rows[:, t, :], out_offset=None, in_=emb,
                        in_offset=bass.IndirectOffsetOnAxis(ap=window_now[:, t:t + 1], axis=0),
                    ).then_inc(rows_gathered, DMA)

            gather(Batch(0))

            def last_of_banks(it, experts):
                last = {it.slot(f"e{e}"): f"e{e}" for e in experts}
                return [x for name in last.values() for x in emptied(it, name)]

            def spread(it, g):
                m = it.moe
                waits = []
                if g == 0:
                    if k_gathers(it):
                        waits += [rows_gathered, it.tok.count(NT * DMA, 2 * NT * DMA)]
                    if it.late:
                        waits += last_of_banks(it, (4, 5, 6))
                    waits += [share_row_in, m.count(4 * DMA, 4 * DMA)]
                else:
                    if it.late:
                        waits += last_of_banks(it, range(QUARTER * g, QUARTER * (g + 1)))
                    if it.late and g == EARLY_SPREADS:
                        waits += [result_ready, it.late.count(1, 1)]
                    waits += [share_spread, m.count(4, g)]
                wait_apart(pool, *waits)
                pool.partition_broadcast(share_all[:, QUARTER * g:QUARTER * (g + 1), :].rearrange("p e t -> p (e t)"),
                                         share_row[32 * g:32 * g + 1, :, :].rearrange("p e t -> p (e t)")
                                         ).then_inc(share_spread, 1)

            def k_gathers(it):
                return it.tok and (it.register is not None or it.tok.number + 1 < BATCHES)

            def iteration(it):
                a, k, m, late = it.attn, it.tok, it.moe, it.late
                if k_gathers(it):
                    gather(Batch(k.number + 1, k.register), it.full("turn4"))
                if a:
                    wait_apart(pool, sum_made, a.count(1, 1), *(emptied(it, "project") if m else []))
                    pool.tensor_copy(sum_now[:], sum_next[:]).then_inc(sum_copied, 1)
                if m:
                    wait_apart(pool, var_f_ready, m.count(1, 1))
                    pool.tensor_tensor(rstd_m[:], var_m[:], minus_half[:, 0:NT], ALU.pow).then_inc(rstd_f_ready, 1)
                if k:
                    pool_tok.start(k)
                    wait_apart(pool, var_k_ready, k.count(1, 1))
                    pool.tensor_tensor(rstd_k[:].rearrange("p a t -> p (a t)"), var_k[:].rearrange("p a t -> p (a t)"),
                                       minus_half[:], ALU.pow).then_inc(rstd_k_ready, 1)
                    pool.wait_ge(a_ready, k.count(1, 1))
                    pool.wait_ge(rstd_k_ready, k.count(1, 1))
                    if k.first():
                        pool.wait_ge(weights_in, 6 * DMA)
                    pool_tok.mark(pool.tensor_tensor(n_hat[:], a_twice[:, :, 0, :],
                                                     rstd_k[:, 1, :, None].to_broadcast([P, NT, C]), ALU.mult))
                    pool_tok.wait(pool)
                    pool_tok.mark(pool.tensor_tensor(n_hat[:], n_hat[:], ln_g[:, None, :].to_broadcast([P, NT, C]), ALU.mult))
                    pool_tok.wait(pool)
                    pool.tensor_tensor(n_twice[:], n_hat[:, :, None, :].to_broadcast([P, NT, 2, C]),
                                       ln_b[:, None, None, :].to_broadcast([P, NT, 2, C]), ALU.add).then_inc(n_ready, 1)
                    if not k.first():
                        pool.wait_ge(sum_copied, k.count(1))
                    pool_tok.mark(pool.tensor_tensor(sum_next[:], h0[:], a_twice[:, :, 0, :], ALU.add))
                    pool_tok.wait(pool)
                    pool_tok.end()
                    pool.tensor_tensor(sum_next[:], sum_next[:], bf[:, None, :].to_broadcast([P, NT, C]), ALU.add
                                       ).then_inc(sum_made, 1)
                if m:
                    for g in range(EARLY_SPREADS):
                        spread(it, g)
                if late:
                    pool_late.start(late)
                    wait_apart(pool, var_y_ready, late.count(1, 1), *((share_spread, m.count(4, EARLY_SPREADS)) if m else ()))
                    pool.tensor_tensor(rstd_y[:], var_y[:], minus_half[:, 0:NT], ALU.pow).then_inc(rstd_y_ready, 1)
                    pool.wait_ge(y_ready, late.count(1, 1))
                    pool_late.mark(pool.tensor_tensor(y[:], y[:], ffn_g[:, None, :].to_broadcast([P, NT, C]), ALU.mult))
                    pool_late.wait(pool)
                    pool_late.mark(pool.tensor_tensor(y[:], y[:], ffn_b[:, None, :].to_broadcast([P, NT, C]), ALU.add))
                    pool_late.wait(pool)
                    pool_late.end()
                    pool.tensor_tensor(y[:], y[:], h1[:, late.parity], ALU.add).then_inc(result_ready, 1)
                if m:
                    for g in range(EARLY_SPREADS, 4):
                        spread(it, g)
                    wait_apart(pool, share_spread, m.count(4, 4))

            run_iterations(pool, iteration)

        @block.scalar
        def _(act):
            act.dma_start(wc[:].rearrange("p b o -> p (b o)"), conv).then_inc(conv_in, DMA)
            act.dma_start(stage[:, 0:EARLY], by_channel[:, 0:EARLY]).then_inc(early_in, DMA)
            for dst, src in ((vector_rows[:], vectors.to_broadcast([P, vectors.shape[1]])), (halved[:], final), (raw_b1, b1),
                             (stage[:, EARLY:by_channel.shape[1]], by_channel[:, EARLY:]),
                             (w2_sb[:].rearrange("p e o -> p (e o)"), w2), (b2_sb[:], b2)):
                act.dma_start(dst, src).then_inc(weights_in, DMA)

            def copy_out(it, name, dst, src):
                act.wait_ge(bank_full, it.full(name))
                nc.scalar.activation(dst, src, ACT.Copy).then_inc(bank_drained[it.slot(name)], 1)

            def exponentials(b, u, pair):
                if u >= 2 or not b.first():
                    act.wait_ge(unit_summed, b.count(UNITS, u - 1))
                for j in range(2 * pair, 2 * pair + 2):
                    n = GROUP * u + j
                    act.wait_ge(max_ready, b.count(SCORES, n + 1))
                    nc.scalar.activation(probs[:, u % 2, j, :], scores[:, n % BANKS, :], ACT.Exp,
                                         bias=neg_max[:, u % 2, j:j + 1], accum_out=z[:, u % 2, j:j + 1]).then_inc(probs_ready, 1)

            def high_part(it, name, dst, scale=1.0):
                act.wait_ge(bank_full, it.full(name))
                return nc.scalar.activation(dst, bank(it, name), ACT.Copy, scale=scale)

            def step(it, name):
                a, k, m = it.attn, it.tok, it.moe
                if name in ("v0", "v1"):
                    n = int(name[1:])
                    if n == 0 and not a.first():
                        act.wait_ge(v_scaled, a.count(UNITS))
                    copy_out(it, name, v_rows[:, 2 * n:2 * n + 2, :].rearrange("p t c -> p (t c)"), bank(it, name))
                elif name in ("turn0", "turn1", "turn2", "turn3"):
                    copy_out(it, name, turned[:, int(name[4:]), :], bank(it, name))
                elif name == "turn4":
                    copy_out(it, name, turned[0:C, 4, :], bank(it, name)[0:C, :])
                elif name in ("conv0", "conv1"):
                    half = slice(0, C) if name == "conv0" else slice(C, P)
                    copy_out(it, name, conv_t[half, :], bank(it, name)[half, :])
                elif name == "rows":
                    if not k.first():
                        act.wait_ge(sum_made, k.count(1))
                    copy_out(it, name, h0[:].rearrange("p t c -> p (t c)"), bank(it, name)[:, 0:NT * C])
                elif name == "turn_f":
                    high_part(it, name, f_split[:, m.parity])
                    nc.scalar.activation(f_ones[0:C, m.parity], bank(it, name)[0:C, :], ACT.Copy).then_inc(high_f, 1)
                elif name in ("gate0", "gate1"):
                    g = int(name[4:])
                    if a.first():
                        act.wait_ge(weights_made, 1)
                    elif name == GATES[0]:
                        act.wait_ge(gated_ready, a.count(GROUPS))
                    act.wait_ge(bank_full, it.full(name))
                    nc.scalar.activation(gate[:, g, :], bank(it, name), ACT.Tanh, bias=half_bg[:, g:g + 1],
                                         scale=0.5).then_inc(bank_drained[it.slot(name)], 1)
                elif name == "e_gap":
                    act.wait_ge(gap_ready, m.count(1, 1))
                    nc.scalar.activation(e_gap[:], gap[:], ACT.Exp).then_inc(e_gap_ready, 1)
                elif name in ("turn_a", "turn_n"):
                    high_part(it, name, (a_split if name == "turn_a" else n_split)[:]).then_inc(high_k, 1)
                elif name == "turn_c":
                    if not m.first():
                        act.wait_ge(share_row_in, m.count(4 * DMA))
                    copy_out(it, name, share_t, bank(it, name)[0:EXPERTS, :])
                elif name in ("q0", "q1"):
                    g = int(name[1:])
                    if not k.first():
                        act.wait_ge(scratch_in[g], k.count(4 * DMA))
                    high_part(it, name, qk_flat[:, g, 0, :], SCALE).then_inc(high_k, 1)
                elif name in ("k0", "k1"):
                    high_part(it, name, qk_flat[:, int(name[1:]), 2, :]).then_inc(high_k, 1)
                else:
                    assert name == "moe_t"
                    act.wait_ge(experts_summed, it.late.count(1, 1))
                    nc.scalar.activation(moe_t[:], experts_sum[:], ACT.Copy).then_inc(moe_t_ready, 1)

            def iteration(it):
                for s in range(2 * UNITS):
                    if it.attn:
                        exponentials(it.attn, s // 2, s % 2)
                    for name in steps(SCALAR_SLOTS, s, it.parts):
                        step(it, name)

            run_iterations(act, iteration)

        @block.vector
        def _(dve):
            vector_setup.start(Batch(0))
            mark = vector_setup.mark

            def wait():
                vector_setup.wait(dve)

            mark(dve.memset(turned[C:P, BLOCKS - 1, :], 1.0))
            mark(dve.memset(f_ones[C:C + BIAS_ROWS].rearrange("p a t -> p (a t)").bitcast(F32), 1.0))
            dve.wait_ge(x_in, 2 * DMA)
            mark(dve.tensor_scalar(windows[:], windows[:], REACH, 0, ALU.subtract, ALU.max))
            wait()
            dve.tensor_scalar(windows[:], windows[:], VOCAB - TAPS, None, ALU.min).then_inc(windows_made, 1)
            dve.wait_ge(consts_made, 1)
            ids = edge_ids[:, 0:1]
            mark(dve.tensor_copy(edge_ids[:, 1:2], ids.bitcast(I32)))
            mark(dve.tensor_copy(same[:, 0, :], expert_ids[:].bitcast(I32)))
            wait()
            mark(dve.tensor_copy(expert_ids[:], same[:, 0, :]))
            mark(dve.tensor_scalar(ids, edge_ids[:, 1:2], REACH - 0.5, VOCAB - EDGES, ALU.is_ge, ALU.mult))
            wait()
            mark(dve.tensor_tensor(ids, ids, edge_ids[:, 1:2], ALU.add))
            mark(dve.tensor_tensor(halves[:], ident[:, 0:C], ident[:, C:P], ALU.add))
            dve.wait_ge(edges_in, DMA)
            dve.tensor_tensor(edge_a, edge_a, edge_b, ALU.subtract).then_inc(edge_diff, 1)

            def split(pairs):
                for hi, lo, raw in pairs:
                    mark(dve.tensor_copy(hi, raw))
                wait()
                for hi, lo, raw in pairs:
                    rows = lo.shape[0]
                    last = dve.tensor_tensor(lo, raw[0:rows], hi[0:rows], ALU.subtract)
                    mark(last) if lo is not pairs[-1][1] else None
                return last

            dve.wait_ge(early_in, DMA)
            split(((w_qkv_hi[:], w_qkv_lo[:], raw_qkv), (w_gate_hi[:], w_gate_lo[:], raw_gate))).then_inc(early_split, 1)
            dve.wait_ge(edge_turned, 1)
            full = BLOCKS - 1
            dve.tensor_copy(edge_t[:, 0:full, :], attended[:, 0:full * EDGES].rearrange("p (k e) -> p k e", e=EDGES)
                            ).then_inc(edge_turned_in, 1)
            dve.tensor_copy(edge_t[0:C, full, :], attended[0:C, full * EDGES:BLOCKS * EDGES]).then_inc(edge_turned_in, 1)
            dve.wait_ge(edge_conv, 1)
            dve.tensor_copy(wc[C:C + EDGES, 4, :], experts_sum[C:C + EDGES, 0:C]).then_inc(edge_weights_in, 1)

            def late_weights():
                dve.wait_ge(weights_in, 6 * DMA)
                dve.tensor_copy(b1_hi, raw_b1).then_inc(bias_parts, 1)
                dve.wait_ge(bias_parts, 1)
                dve.tensor_tensor(b1_lo, raw_b1, b1_hi, ALU.subtract).then_inc(bias_parts, 1)
                mark(dve.tensor_scalar(halved[:], halved[:], 0.5, None, ALU.mult))
                split(((router_hi[:], router_lo[:], raw_router),
                       (w1_hi[:].rearrange("p e f -> p (e f)"), w1_lo[0:C].rearrange("p e f -> p (e f)"), raw_w1))
                      ).then_inc(weights_made, 1)

            def maxima(b, u, pair):
                for j in range(2 * pair, 2 * pair + 2):
                    n = GROUP * u + j
                    dve.wait_ge(scores_ready, b.count(SCORES, n + 1))
                    dve.tensor_reduce(neg_max[:, u % 2, j:j + 1], scores[:, n % BANKS, :], X_AXIS, ALU.max, negate=True
                                      ).then_inc(max_ready, 1)

            def scale_values(it, b, u):
                dve.wait_ge(probs_ready, b.count(SCORES, GROUP * (u + 1)))
                if u >= 2 or not b.first():
                    dve.wait_ge(unit_summed, b.count(UNITS, u - 1))
                dve.reciprocal(inv_z[:, u % 2, :], z[:, u % 2, :]).then_inc(inverse_made, 1)
                yield
                if u == 0:
                    drained(dve, it, "v0")
                    drained(dve, it, "v1")
                dve.wait_ge(inverse_made, b.count(UNITS, u + 1))
                g, t = divmod(u, NT)
                dve.tensor_tensor(v_scaled_sb[:, u % 2], v_rows[:, t, g * P:(g + 1) * P].rearrange("p (h d) -> p h d", d=D),
                                  inv_z[:, u % 2, :, None].to_broadcast([P, GROUP, D]), ALU.mult).then_inc(v_scaled, 1)

            def apply_gate(it, b, g):
                dve.wait_ge(unit_summed, b.count(UNITS, NT * (g + 1)))
                if g == 0:
                    drained(dve, it, "gate0")
                    drained(dve, it, "gate1")
                dve.scalar_tensor_tensor(gate[:, g, :], gate[:, g, :], 1.0, attended[:], ALU.add, ALU.mult
                                         ).then_inc(gated_ready, 1)

            def statistics(order, src, stats, mean):
                for t in range(NT):
                    order.mark(dve.bn_stats(stats[:, t, :], src[:, t, :]))
                yield
                wait_apart(dve, order.sem, order.value())
                for t in range(NT):
                    order.mark(dve.bn_aggr(mean[:, t, :], stats[:, t, :]))
                yield
                order.wait(dve)

            def normalise(order, ready, dst, src, mean, rstd):
                for t in range(NT):
                    one = dve.tensor_scalar(dst(t), src(t), mean[:, t, 0:1], rstd(t), ALU.subtract, ALU.mult)
                    if t < NT - 1:
                        order.mark(one)
                    else:
                        one.then_inc(ready, 1)
                    if t == NT // 2 - 1:
                        yield

            def twice(tile, t):
                return tile[:, t, None, :].to_broadcast([P, 2, C])

            def low_part(it, name, dst, high, scale=None):
                src = bank(it, name)[C:P, :] if scale is None else bank(it, name)
                if scale is None or scale == 1.0:
                    ins = dve.tensor_tensor(dst, src, high, ALU.subtract)
                else:
                    ins = dve.scalar_tensor_tensor(dst, src, scale, high, ALU.mult, ALU.subtract)
                ins.then_inc(bank_drained[it.slot(name)], 1)

            def mark_edges(k):
                dve.wait_ge(x_edge_in, k.count(DMA, DMA))
                if not k.first():
                    dve.wait_ge(rstd_k_ready, k.count(1))
                dve.tensor_scalar(turned[C:C + EDGES, 4, :].rearrange("e (t p) -> e p t", t=NT),
                                  x_edge[C:C + EDGES, :].rearrange("e (p t) -> e p t", t=NT),
                                  edge_ids[C:C + EDGES, 0:1], None, ALU.is_equal).then_inc(edges_marked, 1)

            def statistics_k(it):
                k = it.tok
                o = vector_tok
                o.start(k)
                drained(dve, it, "rows")
                yield from statistics(o, h0, stats_k, mean_k)
                var = mean_k[:, :, 1]
                o.mark(dve.tensor_scalar(var_k[:, 0, :], var, EPS, None, ALU.add))
                yield
                o.wait(dve)
                o.mark(dve.reciprocal(inv_k[:], var_k[:, 0, :]))
                yield
                o.wait(dve)
                o.mark(dve.tensor_tensor(inv_k[:], inv_k[:], var, ALU.mult))
                yield
                o.wait(dve)
                dve.tensor_scalar(var_k[:, 1, :], inv_k[:], EPS, None, ALU.add).then_inc(var_k_ready, 1)

            def norm_a(it):
                k, o = it.tok, vector_tok
                dve.wait_ge(rstd_k_ready, k.count(1, 1))
                if not k.first():
                    dve.wait_ge(sum_made, k.count(1))
                yield from normalise(o, a_ready, lambda t: a_twice[:, t], lambda t: twice(h0, t), mean_k,
                                     lambda t: rstd_k[:, 0, t:t + 1])
                o.end()

            def norm_f_statistics(it):
                m = it.moe
                o = vector_moe
                o.start(m)
                dve.wait_ge(bank_full, it.full("project"))
                dve.wait_ge(sum_copied, m.count(1, 1))
                if m.register is not None or m.number >= 2:
                    dve.wait_ge(result_ready, m.count(1, -1))
                dve.tensor_tensor(h1[:, m.parity].rearrange("p t c -> p (t c)"), bank(it, "project")[:, 0:NT * C],
                                  sum_now[:].rearrange("p t c -> p (t c)"), ALU.add).then_inc(bank_drained[it.slot("project")], 1)
                yield
                drained(dve, it, "project")
                yield from statistics(o, h1[:, m.parity], stats_m, mean_m)
                dve.tensor_scalar(var_m[:], mean_m[:, :, 1], EPS, None, ALU.add).then_inc(var_f_ready, 1)

            def norm_f(it):
                m = it.moe
                dve.wait_ge(rstd_f_ready, m.count(1, 1))
                yield from normalise(vector_moe, f_ready, lambda t: f_twice[:, m.parity, t], lambda t: twice(h1[:, m.parity], t),
                                     mean_m, lambda t: rstd_m[:, t:t + 1])

            wide = [P, NT, EXPERTS]

            def best_two(it):
                m = it.moe
                o = vector_moe
                dve.wait_ge(bank_full, it.full("router"))
                dve.tensor_tensor(logits[:], bank(it, "router")[:, 0:NT * EXPERTS].rearrange("p (t e) -> p t e", e=EXPERTS),
                                  router_bias[:, None, :].to_broadcast(wide), ALU.add).then_inc(bank_drained[it.slot("router")], 1)
                yield
                drained(dve, it, "router")

                def best(src, top, hot):
                    o.mark(dve.tensor_reduce(top[:], src[:], X_AXIS, ALU.max))
                    yield
                    o.wait(dve)
                    o.mark(dve.tensor_tensor(same[:], src[:], top[:, :, None].to_broadcast(wide), ALU.is_equal))
                    yield
                    o.wait(dve)
                    o.mark(dve.tensor_tensor(cand[:], same[:], expert_ids[:, None, :].to_broadcast(wide), ALU.mult))
                    yield
                    o.wait(dve)
                    o.mark(dve.tensor_reduce(which[:], cand[:], X_AXIS, ALU.min))
                    yield
                    o.wait(dve)
                    o.mark(dve.tensor_tensor(hot[:], expert_ids[:, None, :].to_broadcast(wide),
                                             which[:, :, None].to_broadcast(wide), ALU.is_equal))
                    yield
                    o.wait(dve)

                yield from best(logits, top1, first_hot)
                o.mark(dve.scalar_tensor_tensor(logits2[:], first_hot[:], LOWER, logits[:], ALU.mult, ALU.add))
                yield
                o.wait(dve)
                yield from best(logits2, top2, second_hot)
                dve.tensor_tensor(gap[:], top2[:], top1[:], ALU.subtract).then_inc(gap_ready, 1)

            def share_out(it):
                m, o = it.moe, vector_moe
                dve.wait_ge(e_gap_ready, m.count(1, 1))
                o.mark(dve.tensor_scalar(den[:], e_gap[:], 1.0, None, ALU.add))
                yield
                o.wait(dve)
                o.mark(dve.reciprocal(wt1[:], den[:]))
                yield
                o.wait(dve)
                o.mark(dve.tensor_tensor(wt2[:], e_gap[:], wt1[:], ALU.mult))
                o.mark(dve.tensor_tensor(same[:], first_hot[:], wt1[:, :, None].to_broadcast(wide), ALU.mult))
                yield
                o.wait(dve)
                o.mark(dve.tensor_tensor(cand[:], second_hot[:], wt2[:, :, None].to_broadcast(wide), ALU.mult))
                yield
                o.wait(dve)
                dve.tensor_tensor(share[:], same[:], cand[:], ALU.add).then_inc(share_ready, 1)

            def expert(it, e):
                m = it.moe if e < FIRST_EXPERTS else it.late
                dve.wait_ge(bank_full, it.full(f"e{e}"))
                if e % QUARTER == 0 or e < FIRST_EXPERTS:
                    dve.wait_ge(share_spread, m.count(4, e // QUARTER + 1))
                dve.scalar_tensor_tensor(hidden[:, e % 3, :], bank(it, f"e{e}"), 0.0, share_all[:, e, :], ALU.max, ALU.mult
                                         ).then_inc(bank_drained[it.slot(f"e{e}")], 1)

            def final_statistics(it):
                late, o = it.late, vector_late
                o.start(late)
                if not late.first():
                    dve.wait_ge(stored, late.count(DMA))
                dve.wait_ge(bank_full, it.full("sum"))
                dve.tensor_tensor(y[:], bank(it, "sum")[:, 0:NT * C].rearrange("p (t c) -> p t c", c=C),
                                  f_twice[:, late.parity, :, 0, :], ALU.add).then_inc(bank_drained[it.slot("sum")], 1)
                yield
                drained(dve, it, "sum")
                yield from statistics(o, y, stats_y, mean_y)
                dve.tensor_scalar(var_y[:], mean_y[:, :, 1], EPS, None, ALU.add).then_inc(var_y_ready, 1)

            def final_norm(it):
                late, o = it.late, vector_late
                dve.wait_ge(rstd_y_ready, late.count(1, 1))
                yield from normalise(o, y_ready, lambda t: y[:, t, :], lambda t: y[:, t, :], mean_y, lambda t: rstd_y[:, t:t + 1])
                o.end()

            def scale_units(it):
                for u in range(UNITS - 1):
                    yield from scale_values(it, it.attn, u)
                    yield

            def scale_last_unit(it):
                yield from scale_values(it, it.moe, UNITS - 1)

            chains = {"scale": scale_units, "last_unit": scale_last_unit, "h1": norm_f_statistics, "norm_f": norm_f,
                      "statistics_k": statistics_k, "norm_a": norm_a, "best_two": best_two, "share_out": share_out,
                      "statistics_y": final_statistics, "norm_y": final_norm}

            def step(it, name):
                a, k, m, late = it.attn, it.tok, it.moe, it.late
                if name in chains:
                    if name not in it.begun:
                        it.begun[name] = chains[name](it)
                    next(it.begun[name], None)
                elif name[0] == "e":
                    expert(it, int(name[1:]))
                elif name in ("gated0", "gated1"):
                    g = int(name[5:])
                    apply_gate(it, a if g == 0 else m, g)
                elif name == "marks":
                    mark_edges(k)
                elif name == "turn_f":
                    dve.wait_ge(high_f, m.count(1, 1))
                    low_part(it, name, f_split[C:P, m.parity], f_split[C:P, m.parity])
                elif name in ("turn_a", "turn_n"):
                    first = name == "turn_a"
                    dve.wait_ge(high_k, k.count(6, 1 if first else 2))
                    half = (a_split if first else n_split)[C:P, :]
                    low_part(it, name, half, half)
                elif name in ("q0", "q1", "k0", "k1"):
                    g, side = int(name[1:]), "qk".index(name[0])
                    dve.wait_ge(high_k, k.count(6, 3 + 2 * g + side))
                    low_part(it, name, qk_flat[:, g, 2 * side + 1, :], qk_flat[:, g, 2 * side, :], (SCALE, 1.0)[side])
                else:
                    assert False, name

            def iteration(it):
                a = it.attn
                if a and a.first():
                    late_weights()
                for s in range(2 * UNITS):
                    u, pair = divmod(s, 2)
                    if a:
                        maxima(a, u, pair)
                    for name in steps(VECTOR_SLOTS, s, it.parts):
                        step(it, name)
                for chain in it.begun.values():
                    assert next(chain, "complete") == "complete"

            run_iterations(dve, iteration)

        @block.tensor
        def _(pe):
            def edge_weights():
                pe.wait_ge(consts_made, 1)
                pe.wait_ge(edge_diff, 1)
                for k in range(BLOCKS):
                    rows = min(P, WINDOW - P * k)
                    last = pe.transpose(attended[0:rows, EDGES * k:EDGES * (k + 1)], edge_a[:, P * k:P * k + rows],
                                        ident[0:EDGES, 0:EDGES])
                last.then_inc(edge_turned, 1)
                pe.wait_ge(edge_turned_in, 2)
                pe.wait_ge(conv_in, DMA)
                for k in range(BLOCKS):
                    rows = min(P, WINDOW - P * k)
                    last = pe.matmul(experts_sum[C:C + EDGES, 0:C], edge_t[0:rows, k, :], wc[0:rows, k, :],
                                     start=(k == 0), stop=(k == BLOCKS - 1))
                last.then_inc(edge_conv, 1)

            pe.wait_ge(consts_made, 1)

            def take(it, name):
                position = it.position[name]
                assert position == it.next_use, name
                it.next_use += 1
                if it.register is not None or position >= BANKS:
                    value = it.drained(position - BANKS)
                    if name == "turn4":
                        wait_apart(pe, bank_drained[position % BANKS], value)
                    else:
                        pe.wait_ge(bank_drained[position % BANKS], value)
                return bank(it, name)

            def parts(dst, hi, lo, rhs, n=1):
                pe.matmul(dst, hi, rhs, start=True, stop=False)
                return pe.matmul(dst, lo, rhs, start=False, stop=True)

            def query_key(b, n):
                u, j = divmod(n, GROUP)
                g, t = divmod(u, NT)
                if t == 0 and j == 0:
                    pe.wait_ge(stack_in[g], b.count(5 * DMA, 5 * DMA))
                if n >= BANKS:
                    pe.wait_ge(probs_ready, b.count(SCORES, n - BANKS + 1))
                elif not b.first():
                    before = max(x for x in range(SCORES) if x % BANKS == n)
                    pe.wait_ge(probs_ready, b.count(SCORES, before + 1 - SCORES))
                pe.matmul(scores[:, n % BANKS, :], q_stack[:, GROUP * g + j, P * t:P * (t + 1)], k_stack[:, GROUP * g + j, :],
                          start=True, stop=True).then_inc(scores_ready, 1)

            def sum_queries(b, u):
                g, t = divmod(u, NT)
                pe.wait_ge(v_scaled, b.count(UNITS, u + 1))
                if t == 0 and (g > 0 or not b.first()):
                    pe.wait_ge(gated_ready, b.count(GROUPS, g))
                for j in range(GROUP):
                    last = pe.matmul(attended[D * j:D * (j + 1), :], v_scaled_sb[:, u % 2, j, :], probs[:, u % 2, j, :],
                                     start=(t == 0), stop=(t == NT - 1), skip_group_check=True)
                last.then_inc(unit_summed, 1)

            def turn_rows(it, name, tile, rows=P):
                dst = take(it, name)
                for t in range(NT):
                    last = pe.transpose(dst[0:rows, P * t:P * (t + 1)], tile(t), ident[:])
                last.then_inc(bank_full, 1)

            def values(it, n):
                dst = take(it, f"v{n}")
                v = slice(2 * INNER, 3 * INNER)
                for j in range(2):
                    rows = n_split[:, P * (2 * n + j):P * (2 * n + j + 1)]
                    half = dst[:, INNER * j:INNER * (j + 1)]
                    pe.matmul(half, rows, w_qkv_hi[:, v], start=True, stop=False)
                    last = pe.matmul(half, rows, w_qkv_lo[:, v], start=False, stop=True)
                last.then_inc(bank_full, 1)

            def convolution(it, half):
                dst = take(it, f"conv{half}")
                for k in range(half, BLOCKS, 2):
                    rows = P if k < BLOCKS - 1 else C + EDGES + 1
                    last = pe.matmul(dst[C * half:C * (half + 1), :], wc[0:rows, k, :], turned[0:rows, k, :],
                                     start=(k == half), stop=(k + 2 >= BLOCKS), skip_group_check=True)
                last.then_inc(bank_full, 1)

            def add_halves(it, name, tile):
                dst = take(it, name)
                for t in range(NT):
                    last = pe.matmul(dst[:, C * t:C * (t + 1)], tile[:, P * t:P * (t + 1)], halves[:], start=True, stop=True)
                last.then_inc(bank_full, 1)

            def project(it):
                dst = take(it, "project")
                for t in range(NT):
                    for g in range(GROUPS):
                        last = pe.matmul(dst[:, C * t:C * (t + 1)], gate[:, g, P * t:P * (t + 1)], half_wf[:, g, :],
                                         start=(g == 0), stop=(g == GROUPS - 1))
                last.then_inc(bank_full, 1)

            def router(it):
                dst = take(it, "router")
                for t in range(NT):
                    rows = f_split[:, it.moe.parity, P * t:P * (t + 1)]
                    cols = dst[:, EXPERTS * t:EXPERTS * (t + 1)]
                    pe.matmul(cols, rows, router_hi[:], start=True, stop=False)
                    last = pe.matmul(cols, rows, router_lo[:], start=False, stop=True)
                last.then_inc(bank_full, 1)

            def expert_out(it, e, positions):
                position = positions[f"e{e}"]
                pe.wait_ge(bank_drained[position % BANKS], it.drained(position))
                last = pe.matmul(experts_sum[C * (e % 2):C * (e % 2 + 1), :], w2_sb[:, e, :], hidden[:, e % 3, :],
                                 start=(e == 1), stop=(e >= EXPERTS - 2), skip_group_check=True)
                if e == EXPERTS - 1:
                    last.then_inc(experts_summed, 1)

            def expert(it, e):
                m = it.moe if e < FIRST_EXPERTS else it.late
                dst = take(it, f"e{e}")
                pe.matmul(dst, w1_hi[:, e, :], f_split[:, m.parity], start=True, stop=False)
                pe.matmul(dst, w1_lo[:, e, :], f_ones[:, m.parity], start=False, stop=True).then_inc(bank_full, 1)
                if e == 0:
                    if not m.first():
                        pe.wait_ge(moe_t_ready, m.count(1))
                    pe.matmul(experts_sum[0:C, :], b2_sb[:], share_t, start=True, stop=False, skip_group_check=True)
                if e >= LAG:
                    before = e >= FIRST_EXPERTS > e - LAG
                    expert_out(it, e - LAG, it.position_before if before else it.position)

            def step(it, name):
                a, k, m, late = it.attn, it.tok, it.moe, it.late
                if name[0] == "e":
                    if name == "e0":
                        drained(pe, it, "turn_c")
                    expert(it, int(name[1:]))
                elif name in ("v0", "v1"):
                    values(it, int(name[1:]))
                elif name in ("turn0", "turn1", "turn2", "turn3"):
                    n = int(name[4:])
                    if n == 0:
                        pe.wait_ge(rows_gathered, k.count(NT * DMA, NT * DMA))
                    turn_rows(it, name, lambda t: gathered_rows[:, t, P * n:P * (n + 1)])
                elif name == "turn4":
                    turn_rows(it, name, lambda t: gathered_rows[:, t, 4 * P:WINDOW], C)
                elif name == "last_unit":
                    sum_queries(m, UNITS - 1)
                elif name == "project":
                    pe.wait_ge(gated_ready, m.count(GROUPS, GROUPS))
                    project(it)
                elif name == "conv1":
                    if k.first():
                        edge_weights()
                    drained(pe, it, "turn3")
                    convolution(it, 1)
                elif name == "conv0":
                    pe.wait_ge(edges_marked, k.count(1, 1))
                    if k.first():
                        pe.wait_ge(edge_weights_in, 1)
                    drained(pe, it, "turn4")
                    convolution(it, 0)
                elif name == "rows":
                    drained(pe, it, "conv0")
                    drained(pe, it, "conv1")
                    add_halves(it, name, conv_t)
                elif name == "turn_f":
                    pe.wait_ge(f_ready, m.count(1, 1))
                    turn_rows(it, name, lambda t: f_twice[:, m.parity, t].rearrange("p a c -> p (a c)"))
                elif name == "router":
                    drained(pe, it, "turn_f")
                    router(it)
                elif name in ("gate0", "gate1"):
                    w = slice(P * int(name[4:]), P * (int(name[4:]) + 1))
                    parts(take(it, name), w_gate_hi[:, w], w_gate_lo[:, w], a_split[:]).then_inc(bank_full, 1)
                elif name == "turn_a":
                    pe.wait_ge(a_ready, k.count(1, 1))
                    turn_rows(it, name, lambda t: a_twice[:, t].rearrange("p a c -> p (a c)"))
                elif name == "turn_c":
                    pe.wait_ge(share_ready, m.count(1, 1))
                    turn_rows(it, name, lambda t: share[:, t, :], EXPERTS)
                elif name == "turn_n":
                    pe.wait_ge(n_ready, k.count(1, 1))
                    turn_rows(it, name, lambda t: n_twice[:, t].rearrange("p a c -> p (a c)"))
                elif name in ("q0", "q1", "k0", "k1"):
                    first = INNER * "qk".index(name[0]) + P * int(name[1:])
                    w = slice(first, first + P)
                    if name == "q0":
                        if k.first():
                            pe.wait_ge(early_split, 1)
                        drained(pe, it, "turn_n")
                    parts(take(it, name), w_qkv_hi[:, w], w_qkv_lo[:, w], n_split[:]).then_inc(bank_full, 1)
                elif name == "out15":
                    for e in range(EXPERTS - LAG, EXPERTS):
                        expert_out(it, e, it.position)
                else:
                    assert name == "sum"
                    pe.wait_ge(moe_t_ready, late.count(1, 1))
                    add_halves(it, name, moe_t)

            def iteration(it):
                a = it.attn
                if it.moe and it.moe.first():
                    pe.wait_ge(weights_made, 1)
                    pe.wait_ge(bias_rows_in, 2 * DMA)
                for s in range(2 * UNITS):
                    if a:
                        for n in range(2 * s + 1 if s else 0, min(2 * s + BANKS, SCORES)):
                            query_key(a, n)
                        if s % 2 == 1 and s > 1:
                            sum_queries(a, s // 2 - 1)
                    for name in steps(TENSOR_SLOTS, s, it.parts):
                        step(it, name)

            run_iterations(pe, iteration)


def kernel(**inputs):
    import numpy as np
    import concourse.bacc as bacc
    from concourse import mybir as mb
    from concourse.bass_utils import run_bass_kernel_spmd as run

    a = {name: np.asarray(value) for name, value in inputs.items()}
    row = lambda *names: np.concatenate([a[name].reshape(1, -1) for name in names], 1)
    ends = np.r_[0:REACH, VOCAB - REACH:VOCAB][:, None]
    taps = np.arange(TAPS)
    cut_off = np.clip(ends - REACH + taps, 0, VOCAB - 1)
    gathered = np.clip(ends - REACH, 0, VOCAB - TAPS) + taps
    conv = np.zeros((BLOCKS * P, C), a["L0_tok_W"].dtype)
    conv[0:WINDOW] = a["L0_tok_W"].transpose(2, 1, 0).reshape(WINDOW, C)
    conv[WINDOW + EDGES] = a["L0_tok_b"]
    by_channel = np.concatenate([a["L0_attn_W_qkv"].T, a["L0_attn_W_gate"].T, a["L0_ffn_gate_w"],
                                 a["L0_ffn_w1"].transpose(1, 0, 2).reshape(C, EXPERTS * F)], 1)
    arrays = {
        "x": a["x"],
        "emb": a["L0_tok_emb"],
        "edges": np.concatenate([a["L0_tok_emb"][rows].reshape(EDGES, WINDOW) for rows in (cut_off, gathered)], 1),
        "conv": conv.reshape(BLOCKS, P, C).transpose(1, 0, 2).reshape(P, BLOCKS * C),
        "by_channel": np.concatenate([by_channel, by_channel], 0),
        "final": np.concatenate([a["L0_attn_W_final"].T.reshape(GROUPS, P, C).transpose(1, 0, 2).reshape(P, GROUPS * C),
                                 a["L0_attn_b_gate"].reshape(GROUPS, P).T], 1),
        "vectors": row("L0_attn_ln_gamma", "L0_attn_ln_beta", "L0_attn_b_final", "L0_ffn_gamma", "L0_ffn_beta", "L0_ffn_gate_b"),
        "b1": row("L0_ffn_b1"),
        "w2": a["L0_ffn_w2"].transpose(1, 0, 2).reshape(F, EXPERTS * C),
        "b2": a["L0_ffn_b2"],
    }
    arrays = {f"in_{name}": np.ascontiguousarray(v) for name, v in arrays.items()}
    nc = bacc.Bacc("TRN2", target_bir_lowering=False, num_devices=1)
    args = [nc.dram_tensor(name, v.shape, mb.dt.from_np(v.dtype), kind="ExternalInput").ap() for name, v in arrays.items()]
    out = nc.dram_tensor("out", (BATCHES, T, C), mb.dt.float32, kind="ExternalOutput").ap()
    tower_kernel(nc, *args, out)
    return run(nc, [arrays], core_ids=[0]).results[0]["out"]
```
